# Optimizing a Trainium2 kernel written in Bass

```python
import numpy as np
import jax
import jax.numpy as jnp

def _softmax(x, axis=-1):
    return jax.nn.softmax(x, axis=axis)

def _gelu(x):
    return jax.nn.gelu(x, approximate=True)

def _silu(x):
    return jax.nn.silu(x)

def _sigmoid(x):
    return jax.nn.sigmoid(x)

def _layernorm(x, axis=-1, eps=1e-05):
    m = jnp.mean(x, axis=axis, keepdims=True)
    v = jnp.var(x, axis=axis, keepdims=True)
    return (x - m) / jnp.sqrt(v + eps)

def _scatter_add(tgt, idx, src, axis=0):
    return tgt.at[idx].add(src)

def _segment_sum(src, seg, n):
    return jax.ops.segment_sum(src, seg, n)
kernel_name = 'mk_audio_tower_d2_tok_audfeat512_r4_9948c1'

def setup_inputs(seed: int=0):
    np.random.seed(seed)
    _w = jnp.asarray

    def _rec_inputs():
        import jax
        import jax.numpy as jnp
        _rk = jax.random.key(seed)
        x = -3.53888e-05 + 1.00021 * jax.random.normal(jax.random.fold_in(_rk, 1), (4, 750, 23), jnp.float32)
        return x
    x = _rec_inputs()

    def _L0_tok_setup():
        import jax, jax.numpy as jnp
        import numpy as np
        CONTEXT = 5
        DILATION = 1
        BN_EPS = 1e-05

        def _tdnn_forward(x, W, b, gamma, beta):
            B, T, D = x.shape
            L = T - (CONTEXT - 1) * DILATION
            frames = jnp.stack([jax.lax.dynamic_slice_in_dim(x, k * DILATION, L, axis=1) for k in range(CONTEXT)], axis=2)
            patches = frames.reshape(B, L, CONTEXT * D)
            y = jnp.einsum('blf,of->blo', patches, W) + b
            y = jax.nn.relu(y)
            mean = jnp.mean(y, axis=(0, 1))
            var = jnp.var(y, axis=(0, 1))
            y = (y - mean) * jax.lax.rsqrt(var + BN_EPS) * gamma + beta
            return y
        key = jax.random.key(seed)
        k1, k2, k3 = jax.random.split(key, 3)
        B, T, D, O = (64, 1024, 23, 128)
        x = jax.random.normal(k1, (B, T, D), dtype=jnp.float32)
        fan_in = D * CONTEXT
        bound = 1.0 / np.sqrt(fan_in)
        W = jax.random.uniform(k2, (O, fan_in), dtype=jnp.float32, minval=-bound, maxval=bound)
        b = jax.random.uniform(k3, (O,), dtype=jnp.float32, minval=-bound, maxval=bound)
        gamma = jnp.ones((O,), dtype=jnp.float32)
        beta = jnp.zeros((O,), dtype=jnp.float32)
        return {'x': x, 'W': W, 'b': b, 'gamma': gamma, 'beta': beta}
    _L0_tok_all = _L0_tok_setup()
    _L0_tok_in = {k: v for k, v in _L0_tok_all.items() if k in ('W', 'b', 'gamma', 'beta')}
    del _L0_tok_all

    def _L0_attn_setup():
        import jax, jax.numpy as jnp
        import numpy as np
        B, T, H, N = (4, 512, 128, 8)
        THETA = 10000.0
        PERIOD, RET_ORDER = (3, 2)

        def _rope(z, cos, sin):
            b, t, c = z.shape
            z = z.reshape(b, t, c // 2, 2)
            zr = z[..., 0] * cos - z[..., 1] * sin
            zi = z[..., 0] * sin + z[..., 1] * cos
            return jnp.stack([zr, zi], axis=-1).reshape(b, t, c)
        key = jax.random.key(seed)
        ks = jax.random.split(key, 9)
        s = 0.02
        return {'x': jax.random.normal(ks[0], (B, T, H), dtype=jnp.float32), 'Wq': jax.random.normal(ks[1], (H, H), dtype=jnp.float32) * s, 'bq': jax.random.normal(ks[2], (H,), dtype=jnp.float32) * s, 'Wk': jax.random.normal(ks[3], (H, H), dtype=jnp.float32) * s, 'bk': jax.random.normal(ks[4], (H,), dtype=jnp.float32) * s, 'Wv': jax.random.normal(ks[5], (H, H), dtype=jnp.float32) * s, 'bv': jax.random.normal(ks[6], (H,), dtype=jnp.float32) * s, 'Wo': jax.random.normal(ks[7], (H, H), dtype=jnp.float32) * s, 'bo': jax.random.normal(ks[8], (H,), dtype=jnp.float32) * s}
    _L0_attn_all = _L0_attn_setup()
    _L0_attn_in = {k: v for k, v in _L0_attn_all.items() if k in ('Wq', 'bq', 'Wk', 'bk', 'Wv', 'bv', 'Wo', 'bo')}
    del _L0_attn_all

    def _L0_ffn_setup():
        import jax, jax.numpy as jnp
        import numpy as np
        import math
        D_MODEL = 128
        N_EXPERTS = 128
        TOP_K = 8
        N_HEADS = 8
        D_KEYS = 128
        HALF = D_KEYS // 2
        N_BATCH, T_SEQ = (2, 512)
        key = jax.random.key(seed)
        k1, k2, k3, k4, k5, k6 = jax.random.split(key, 6)
        queries = jax.random.normal(k1, (N_BATCH, T_SEQ, D_MODEL), dtype=jnp.float32)
        bound_q = 1.0 / math.sqrt(D_MODEL)
        Wq = jax.random.uniform(k2, (N_HEADS * D_KEYS, D_MODEL), minval=-bound_q, maxval=bound_q, dtype=jnp.float32)
        bq = jax.random.uniform(k3, (N_HEADS * D_KEYS,), minval=-bound_q, maxval=bound_q, dtype=jnp.float32)
        bound_k = 1.0 / math.sqrt(HALF)
        keys = jax.random.uniform(k4, (N_HEADS, 2, N_EXPERTS, HALF), minval=-bound_k, maxval=bound_k, dtype=jnp.float32)
        std = D_MODEL ** (-0.5)
        w_down_embed = std * jax.random.normal(k5, (N_EXPERTS * N_EXPERTS, D_MODEL), dtype=jnp.float32)
        w_up_embed = std * jax.random.normal(k6, (N_EXPERTS * N_EXPERTS, D_MODEL), dtype=jnp.float32)
        return {'queries': queries, 'Wq': Wq, 'bq': bq, 'keys': keys, 'w_down_embed': w_down_embed, 'w_up_embed': w_up_embed}
    _L0_ffn_all = _L0_ffn_setup()
    _L0_ffn_in = {k: v for k, v in _L0_ffn_all.items() if k in ('Wq', 'bq', 'keys', 'w_down_embed', 'w_up_embed')}
    del _L0_ffn_all

    def _L1_attn_setup():
        import jax, jax.numpy as jnp
        from jax import lax
        import numpy as np
        N, M, C = (4, 512, 128)
        H, TOPK = (8, 16)
        key = jax.random.key(seed)
        ks = jax.random.split(key, 5)
        s = 0.02
        return {'x': jax.random.normal(ks[0], (N, M, C), jnp.float32), 'conv_w': jax.random.normal(ks[1], (C, 1, 3), jnp.float32) * s, 'conv_b': jnp.zeros((C,), jnp.float32), 'w_qkv': jax.random.normal(ks[2], (C, 3 * C), jnp.float32) * s, 'b_qkv': jnp.zeros((3 * C,), jnp.float32), 'w_o': jax.random.normal(ks[3], (C, C), jnp.float32) * s, 'b_o': jnp.zeros((C,), jnp.float32)}
    _L1_attn_all = _L1_attn_setup()
    _L1_attn_in = {k: v for k, v in _L1_attn_all.items() if k in ('conv_w', 'conv_b', 'w_qkv', 'b_qkv', 'w_o', 'b_o')}
    del _L1_attn_all

    def _L1_ffn_setup():
        import jax, jax.numpy as jnp
        import numpy as np
        K = 2
        key = jax.random.key(seed)
        ks = jax.random.split(key, 6)
        B, T, d, E, dff = (2, 512, 128, 8, 512)
        x = jax.random.normal(ks[0], (B, T, d), dtype=jnp.float32)
        Wg = jax.random.normal(ks[1], (d, E), dtype=jnp.float32) * 0.02
        W1 = jax.random.normal(ks[2], (E, d, dff), dtype=jnp.float32) * 0.02
        b1 = jnp.zeros((E, dff), dtype=jnp.float32)
        W2 = jax.random.normal(ks[3], (E, dff, d), dtype=jnp.float32) * 0.02
        b2 = jnp.zeros((E, d), dtype=jnp.float32)
        return {'x': x, 'Wg': Wg, 'W1': W1, 'b1': b1, 'W2': W2, 'b2': b2}
    _L1_ffn_all = _L1_ffn_setup()
    _L1_ffn_in = {k: v for k, v in _L1_ffn_all.items() if k in ('Wg', 'W1', 'b1', 'W2', 'b2')}
    del _L1_ffn_all
    return {'x': x, 'L0_tok_W': _L0_tok_in['W'], 'L0_tok_b': _L0_tok_in['b'], 'L0_tok_gamma': _L0_tok_in['gamma'], 'L0_tok_beta': _L0_tok_in['beta'], 'L0_attn_Wq': _L0_attn_in['Wq'], 'L0_attn_bq': _L0_attn_in['bq'], 'L0_attn_Wk': _L0_attn_in['Wk'], 'L0_attn_bk': _L0_attn_in['bk'], 'L0_attn_Wv': _L0_attn_in['Wv'], 'L0_attn_bv': _L0_attn_in['bv'], 'L0_attn_Wo': _L0_attn_in['Wo'], 'L0_attn_bo': _L0_attn_in['bo'], 'L0_ffn_Wq': _L0_ffn_in['Wq'], 'L0_ffn_bq': _L0_ffn_in['bq'], 'L0_ffn_keys': _L0_ffn_in['keys'], 'L0_ffn_w_down_embed': _L0_ffn_in['w_down_embed'], 'L0_ffn_w_up_embed': _L0_ffn_in['w_up_embed'], 'L1_attn_conv_w': _L1_attn_in['conv_w'], 'L1_attn_conv_b': _L1_attn_in['conv_b'], 'L1_attn_w_qkv': _L1_attn_in['w_qkv'], 'L1_attn_b_qkv': _L1_attn_in['b_qkv'], 'L1_attn_w_o': _L1_attn_in['w_o'], 'L1_attn_b_o': _L1_attn_in['b_o'], 'L1_ffn_Wg': _L1_ffn_in['Wg'], 'L1_ffn_W1': _L1_ffn_in['W1'], 'L1_ffn_b1': _L1_ffn_in['b1'], 'L1_ffn_W2': _L1_ffn_in['W2'], 'L1_ffn_b2': _L1_ffn_in['b2']}

def reference(x, L0_tok_W, L0_tok_b, L0_tok_gamma, L0_tok_beta, L0_attn_Wq, L0_attn_bq, L0_attn_Wk, L0_attn_bk, L0_attn_Wv, L0_attn_bv, L0_attn_Wo, L0_attn_bo, L0_ffn_Wq, L0_ffn_bq, L0_ffn_keys, L0_ffn_w_down_embed, L0_ffn_w_up_embed, L1_attn_conv_w, L1_attn_conv_b, L1_attn_w_qkv, L1_attn_b_qkv, L1_attn_w_o, L1_attn_b_o, L1_ffn_Wg, L1_ffn_W1, L1_ffn_b1, L1_ffn_W2, L1_ffn_b2):
    import jax
    import jax.numpy as jnp

    def _L0_tok_ref(x, W, b, gamma, beta):
        import jax, jax.numpy as jnp
        import numpy as np
        CONTEXT = 5
        DILATION = 1
        BN_EPS = 1e-05

        def _tdnn_forward(x, W, b, gamma, beta):
            B, T, D = x.shape
            L = T - (CONTEXT - 1) * DILATION
            frames = jnp.stack([jax.lax.dynamic_slice_in_dim(x, k * DILATION, L, axis=1) for k in range(CONTEXT)], axis=2)
            patches = frames.reshape(B, L, CONTEXT * D)
            y = jnp.einsum('blf,of->blo', patches, W) + b
            y = jax.nn.relu(y)
            mean = jnp.mean(y, axis=(0, 1))
            var = jnp.var(y, axis=(0, 1))
            y = (y - mean) * jax.lax.rsqrt(var + BN_EPS) * gamma + beta
            return y
        return _tdnn_forward(x, W, b, gamma, beta)

    def _L0_attn_ref(x, Wq, bq, Wk, bk, Wv, bv, Wo, bo):
        import jax, jax.numpy as jnp
        import numpy as np
        B, T, H, N = (4, 512, 128, 8)
        THETA = 10000.0
        PERIOD, RET_ORDER = (3, 2)

        def _rope(z, cos, sin):
            b, t, c = z.shape
            z = z.reshape(b, t, c // 2, 2)
            zr = z[..., 0] * cos - z[..., 1] * sin
            zi = z[..., 0] * sin + z[..., 1] * cos
            return jnp.stack([zr, zi], axis=-1).reshape(b, t, c)
        Bx, Tx, C = x.shape
        D = C // N
        inv_freq = 1.0 / THETA ** (jnp.arange(0, C, 2, dtype=jnp.float32) / C)
        ang = jnp.arange(Tx, dtype=jnp.float32)[:, None] * inv_freq[None, :]
        cos, sin = (jnp.cos(ang), jnp.sin(ang))
        q = x @ Wq + bq
        k = x @ Wk + bk
        q = _rope(q, cos, sin)
        k = _rope(k, cos, sin)
        v = x @ Wv + bv
        q = q.reshape(Bx, Tx, N, D).transpose(0, 2, 1, 3)
        k = k.reshape(Bx, Tx, N, D).transpose(0, 2, 1, 3)
        v = v.reshape(Bx, Tx, N, D).transpose(0, 2, 1, 3)
        scores = jnp.einsum('bntd,bnsd->bnts', q, k) / jnp.float32(D) ** 0.5
        mask = jnp.tril(jnp.ones((Tx, Tx), dtype=bool))
        ret_cols = np.arange(PERIOD + RET_ORDER - 1, Tx, PERIOD)
        mask = mask.at[:, ret_cols].set(False)
        scores = jnp.where(mask[None, None], scores, -jnp.inf)
        att = jax.nn.softmax(scores, axis=-1)
        out = jnp.einsum('bnts,bnsd->bntd', att, v)
        out = out.transpose(0, 2, 1, 3).reshape(Bx, Tx, C)
        return out @ Wo + bo

    def _L0_ffn_ref(queries, Wq, bq, keys, w_down_embed, w_up_embed):
        import jax, jax.numpy as jnp
        import numpy as np
        import math
        D_MODEL = 128
        N_EXPERTS = 128
        TOP_K = 8
        N_HEADS = 8
        D_KEYS = 128
        HALF = D_KEYS // 2
        N_BATCH, T_SEQ = (2, 512)
        N, T, D = queries.shape
        H, E, K = (N_HEADS, N_EXPERTS, TOP_K)
        q_tok = queries.reshape(-1, D)
        qh = q_tok @ Wq.T + bq
        qh = qh.reshape(-1, H, 2, HALF)
        sub_scores = jnp.einsum('nhcf,hcef->nhce', qh, keys)
        s, idx = jax.lax.top_k(sub_scores, K)
        all_scores = (s[:, :, 0, :, None] + s[:, :, 1, None, :]).reshape(-1, H, K * K)
        all_idx = (idx[:, :, 0, :, None] * E + idx[:, :, 1, None, :]).reshape(-1, H, K * K)
        best_s, best_pos = jax.lax.top_k(all_scores, K)
        indices = jnp.take_along_axis(all_idx, best_pos, axis=-1)
        w_down = w_down_embed[indices]
        w_up = w_up_embed[indices]
        x = jnp.einsum('nd,nhkd->nhk', q_tok, w_down)
        x = jax.nn.gelu(x)
        vals = x * jax.nn.softmax(best_s, axis=-1)
        out = jnp.einsum('nhk,nhkd->nd', vals, w_up)
        return out.reshape(N, T, D)

    def _L1_attn_ref(x, conv_w, conv_b, w_qkv, b_qkv, w_o, b_o):
        import jax, jax.numpy as jnp
        from jax import lax
        import numpy as np
        N, M, C = (4, 512, 128)
        H, TOPK = (8, 16)
        n, m, c = x.shape
        h, topk = (H, TOPK)
        d = c // h
        scale = c ** (-0.5)
        pos = lax.conv_general_dilated(x.transpose(0, 2, 1), conv_w, window_strides=(1,), padding='SAME', feature_group_count=c, dimension_numbers=('NCW', 'OIW', 'NCW'))
        pos = pos + conv_b[None, :, None]
        x = x + pos.transpose(0, 2, 1)
        qkv = x @ w_qkv + b_qkv
        q, k, v = jnp.split(qkv, [c, 2 * c], axis=-1)

        def to_heads(t):
            return t.reshape(n, m, h, d).transpose(0, 2, 1, 3).reshape(n * h, m, d)
        q, k, v = (to_heads(q), to_heads(k), to_heads(v))
        qd, kd = (lax.stop_gradient(q), lax.stop_gradient(k))
        logit = jnp.einsum('bmd,bld->bml', qd * scale, kd)
        _, idx = lax.top_k(logit, topk)
        k_sel = jax.vmap(lambda kk, ii: kk[ii])(k, idx)
        v_sel = jax.vmap(lambda vv, ii: vv[ii])(v, idx)
        aw = jnp.einsum('bmd,bmkd->bmk', q * scale, k_sel)
        aw = jax.nn.softmax(aw, axis=-1)
        out = jnp.einsum('bmk,bmkd->bmd', aw, v_sel)
        out = out.reshape(n, h, m, d).transpose(0, 2, 1, 3).reshape(n, m, c)
        return out @ w_o + b_o

    def _L1_ffn_ref(x, Wg, W1, b1, W2, b2):
        import jax, jax.numpy as jnp
        import numpy as np
        K = 2
        logits = jnp.einsum('btd,de->bte', x, Wg)
        probs = jax.nn.softmax(logits, axis=-1)
        top_p, _top_i = jax.lax.top_k(probs, K)
        top_p = top_p / jnp.sum(top_p, axis=-1, keepdims=True)
        b2_sum = jnp.sum(b2, axis=0)
        out = jnp.zeros_like(x)
        for i in range(K):
            w_in = x * top_p[..., i:i + 1]
            h = jax.nn.gelu(jnp.einsum('btd,edf->ebtf', w_in, W1) + b1[:, None, None, :], approximate=False)
            out = out + jnp.einsum('ebtf,efd->btd', h, W2) + b2_sum
        return out
    h = _L0_tok_ref(x, L0_tok_W, L0_tok_b, L0_tok_gamma, L0_tok_beta)
    h = h + _L0_attn_ref(_layernorm(h, axis=-1), L0_attn_Wq, L0_attn_bq, L0_attn_Wk, L0_attn_bk, L0_attn_Wv, L0_attn_bv, L0_attn_Wo, L0_attn_bo)
    h = h + _L0_ffn_ref(_layernorm(h, axis=-1), L0_ffn_Wq, L0_ffn_bq, L0_ffn_keys, L0_ffn_w_down_embed, L0_ffn_w_up_embed)
    h = h + _L1_attn_ref(_layernorm(h, axis=-1), L1_attn_conv_w, L1_attn_conv_b, L1_attn_w_qkv, L1_attn_b_qkv, L1_attn_w_o, L1_attn_b_o)
    h = h + _L1_ffn_ref(_layernorm(h, axis=-1), L1_ffn_Wg, L1_ffn_W1, L1_ffn_b1, L1_ffn_W2, L1_ffn_b2)
    return h

_drawn_inputs = setup_inputs


def setup_inputs(seed=0):
    import zlib

    import numpy as np

    out = dict(_drawn_inputs(seed))
    spreads = {'L0_tok_gamma': (1.0, 0.2),
     'L0_tok_beta': (0.0, 0.1),
     'L1_attn_conv_b': (0.0, 0.8),
     'L1_attn_b_qkv': (0.0, 0.372),
     'L1_attn_b_o': (0.0, 0.1),
     'L1_ffn_b1': (0.0, 0.1),
     'L1_ffn_b2': (0.0, 0.1)}
    factors = {'L0_attn_Wq': 8.0,
     'L0_attn_bq': 8.0,
     'L0_attn_Wk': 8.0,
     'L0_attn_bk': 8.0,
     'L0_attn_Wv': 6.698,
     'L0_attn_bv': 8.0,
     'L0_attn_Wo': 5.674,
     'L0_attn_bo': 2.801,
     'L0_ffn_bq': 2.738,
     'L1_attn_conv_w': 8.0,
     'L1_attn_w_qkv': 3.546,
     'L1_ffn_Wg': 8.0}
    for name, (base, spread) in spreads.items():
        noise = np.random.default_rng([zlib.crc32(name.encode()), seed]).standard_normal(out[name].shape)
        drawn = base * np.exp(spread * noise) if base else spread * noise
        out[name] = jnp.asarray(drawn.astype(out[name].dtype))
    for name, factor in factors.items():
        out[name] = (out[name] * factor).astype(out[name].dtype)
    return out
```

```python
from contextlib import ExitStack

import concourse.bass as bass
from concourse import mybir

F32 = mybir.dt.float32
U32 = mybir.dt.uint32
ALU = mybir.AluOpType
ACT = mybir.ActivationFunctionType
AX = mybir.AxisListType

B, T_IN, D_IN = 4, 750, 23
CONTEXT = 5
T_REAL = T_IN - CONTEXT + 1
C = 128
ROWS = 125
TPB = 6
NT = B * TPB
T_PAD = ROWS * TPB
TOK = B * T_PAD
HALF = T_REAL // 2
H, DH = 8, 16
EPS = 1e-5
KEYS0 = 498
PAIRS0 = (KEYS0 - 2) // 2
KEYS0_PAD = 500
VW = DH + 1
PK_HEADS, PK_TOP = 8, 8
PK_ROWS = PK_HEADS * PK_TOP
RING = 16
NEG = -1.0e30
SCALE0 = DH ** -0.5
SCALE1 = C ** -0.5
EXPERTS, FF = 8, 512
FCH = EXPERTS * FF // C
GROUP = 500
HEADS_PER_BODY = 4
N_LOADS = 12
GELU_A, GELU_B = 0.7978845608028654, 0.044715


def audio_tower(nc, t, stop=99):
    ctx = ExitStack()
    with ctx:
        def sb(name, shape, dt=F32):
            return ctx.enter_context(nc.sbuf_tensor(name, shape, dt))

        def sem(name):
            return ctx.enter_context(nc.semaphore(name))

        h_tok = sb("h_tok", [ROWS, NT, C])
        xn_tok = sb("xn_tok", [ROWS, NT, C])
        xT = sb("xT", [C, TOK])
        o_tok = sb("o_tok", [ROWS, B, TPB, C])
        v_all = sb("v_all", [ROWS, B * H, TPB, VW])
        arena = sb("arena", [C, 16384])
        q_slot = [sb(f"q_slot{s}", [DH, T_PAD]) for s in range(2)]
        k_slot = [sb(f"k_slot{s}", [DH, T_PAD]) for s in range(2)]
        v_slot = [sb(f"v_slot{s}", [ROWS, TPB, VW]) for s in range(2)]
        ident = sb("ident", [C, C])
        iota8 = sb("iota8", [C, PK_TOP])
        ones_row = sb("ones_row", [1, ROWS])
        w1 = sb("w1", [C, FCH, C])
        w2 = sb("w2", [C, FCH, C])
        tokw = sb("tokw", [CONTEXT * D_IN, C])
        cols = sb("cols", [C, 64])
        a0w = sb("a0w", [C, 6, C])
        rows1 = sb("rows1", [1, 4, C])
        pkwq = sb("pkwq", [C, PK_HEADS * C])
        pkkeys = sb("pkkeys", [C, PK_HEADS * C])
        a1w = sb("a1w", [C, 4, C])
        wg = sb("wg", [C, EXPERTS])
        stats = sb("stats", [C, NT, 6])
        mv = sb("mv", [C, NT, 2])
        std = sb("std", [C, NT])
        rstd = sb("rstd", [C, NT])
        bn = sb("bn", [C, 8])
        m16 = sb("m16", [ROWS, 3, 16])
        negmax = sb("negmax", [ROWS, 3])
        recip = sb("recip", [ROWS, 2, TPB])
        qhT = sb("qhT", [C, PK_HEADS, ROWS])
        s8 = sb("s8", [ROWS, 2, H, 8])
        i8 = sb("i8", [ROWS, 2, H, 8], U32)
        i8f = sb("i8f", [ROWS, 2, H, 8])
        pair_s = sb("pair_s", [ROWS, H, 64])
        best = sb("best", [ROWS, H, 8])
        pos = sb("pos", [ROWS, H, 8], U32)
        pos_ij = sb("pos_ij", [ROWS, 2, 64], U32)
        onehot = sb("onehot", [ROWS, 2, 64, 8])
        r_ij = sb("r_ij", [ROWS, 2, 64])
        idx = [sb(f"idx{p}", [C, PK_ROWS], U32) for p in range(2)]
        w_next = sb("w_next", [ROWS, H, 8])
        w_cur = sb("w_cur", [ROWS, 64])
        pk8 = sb("pk8", [ROWS, H])
        q_cur = sb("q_cur", [ROWS, C])
        xdot = sb("xdot", [ROWS, 64])
        gl = sb("gl", [ROWS, 3, 2 * RING])
        vals = sb("vals", [ROWS, 64])
        usum = sb("usum", [ROWS, C])
        lg = sb("lg", [ROWS, NT, EXPERTS])
        lg_m = sb("lg_m", [ROWS, NT])
        top_p = sb("top_p", [ROWS, NT, EXPERTS])
        p_i = sb("p_i", [ROWS, 2, NT])

        COL = dict(tok_b=0, gamma=1, beta=2, bq=3, bqs=4, bk=5, bks=6, conv=7, conv_b=10,
                   l1q=11, l1k=12, pkbq=13, b1=21, b2=53)

        def col(name, i=0):
            return cols[:, COL[name] + i:COL[name] + i + 1]

        bank = [ctx.enter_context(nc.psum_tensor(f"bank{i}", [C, 512], F32)) for i in range(2)]
        psum = ctx.enter_context(nc.psum_tensor("psum", [C, 6 * 512], F32))
        bank += [psum[:, 512 * i:512 * i + 512] for i in range(6)]

        def A(at, n, p=C):
            return arena[0:p, at:at + n]

        q_dram = nc.dram_tensor("q_dram", [B * H, DH, T_PAD], F32, kind="Internal").ap()
        k_dram = nc.dram_tensor("k_dram", [B * H, DH, T_PAD], F32, kind="Internal").ap()

        phase_done = sem("phase_done")
        loaded_tok = sem("loaded_tok")
        loaded_all = sem("loaded_all")
        mm_ready = sem("mm_ready")
        mm_ready_v = sem("mm_ready_v")
        act_ready = sem("act_ready")
        act_ready_pe = sem("act_ready_pe")
        dve_ready = sem("dve_ready")
        dve_to_act = sem("dve_to_act")
        dve_self = sem("dve_self")
        act_self = sem("act_self")
        pool_self = sem("pool_self")
        qk_stored = sem("qk_stored")
        slot_loaded = [sem(f"slot_loaded{s}") for s in range(2)]
        slot_free = [sem(f"slot_free{s}") for s in range(2)]
        s_ready = sem("s_ready")
        s_free = sem("s_free")
        s_masked = sem("s_masked")
        s_replaced = [sem(f"s_replaced{k}") for k in range(2)]
        e_ready = sem("e_ready")
        p_ready = sem("p_ready")
        t_ready = sem("t_ready")
        pt_ready = sem("pt_ready")
        o_ready = sem("o_ready")
        o_free = [sem(f"o_free{s}") for s in range(2)]
        scores_ready = sem("scores_ready")
        scores_free = sem("scores_free")
        idx_ready = sem("idx_ready")
        gathered = [sem(f"gathered{k}") for k in range(4)]
        ring_free = [sem(f"ring_free{k}") for k in range(4)]
        up_ready = sem("up_ready")
        usum_ready = sem("usum_ready")
        usum_free = sem("usum_free")
        q_used = sem("q_used")
        k_used = sem("k_used")
        z_ready = sem("z_ready")
        g_ready = sem("g_ready")
        gs_ready = sem("gs_ready")
        stored = sem("stored")

        phase = {}

        def end_phase(eng):
            phase[eng] = phase.get(eng, 0) + 1
            eng.drain().then_inc(phase_done, 1)
            eng.wait_ge(phase_done, 4 * phase[eng])

        def enter_phase(eng, n):
            eng.wait_ge(phase_done, 4 * n)

        patches = A(0, B * T_REAL, CONTEXT * D_IN).rearrange("p (b n) -> p b n", b=B)
        yT = A(3000, TOK)
        QT, KT = A(0, TOK), A(3000, TOK)
        cosT, sinT = A(6000, T_PAD), A(6750, T_PAD)
        mask0 = A(7500, TPB * KEYS0_PAD, ROWS).rearrange("p (i n) -> p i n", i=TPB)
        rot_q, rot_k = ([A(at, T_PAD), A(at + T_PAD, T_PAD)] for at in (10500, 12500))
        xc = A(12000, KEYS0_PAD)
        sm0 = [A(12000 + 500 * k, 500, ROWS) for k in range(3)]
        pr0 = [A(13500 + 500 * k, 500, ROWS) for k in range(3)]
        pt0 = A(15000, 500, ROWS)
        G = arena[:, :].rearrange("p (k r d) -> p k r d", k=4, r=RING)
        conv_t, conv_x = A(6000, TOK), A(9000, TOK)
        w_a = A(6000, T_PAD, ROWS)
        w_b = [A(750 * (9 + k), T_PAD, ROWS) for k in range(3)]
        e_a = [A(750 * (12 + k), T_PAD, ROWS) for k in range(3)]
        pr1 = [A(750 * (15 + k), T_PAD, ROWS) for k in range(3)]
        pt1 = A(13500, T_PAD, ROWS)
        oT = [A(15000, GROUP), A(15500, GROUP)]
        wT = [A(0, TOK), A(3000, TOK)]
        xs = A(6000, 2 * 2 * 4 * C, ROWS).rearrange("p (j i g c) -> p j i g c", j=2, i=2, g=4)
        g_act = [[A(8100 + 1000 * m + 500 * i, GROUP) for i in range(2)] for m in range(2)]
        g_sum = [A(10100 + 500 * m, GROUP) for m in range(2)]
        yT_ffn = A(11100, GROUP)

        visible = [sum(1 for s in range(T_REAL) if s <= ROWS * i + ROWS - 1 and not (s >= 4 and s % 3 == 1))
                   for i in range(TPB)]
        chunks0 = [-(-v // ROWS) for v in visible]

        block = ctx.enter_context(nc.Block())

        @block.sync
        def _(sp):
            for k in range(CONTEXT):
                sp.dma_start(patches[D_IN * k:D_IN * (k + 1), :, :],
                             t["x"][:, :, k:k + T_REAL]).then_inc(loaded_tok, 16)
            sp.dma_start(tokw[:, :], t["tok_W"]).then_inc(loaded_tok, 16)
            sp.dma_start(cols[:, :], t["cols"]).then_inc(loaded_tok, 16)
            sp.dma_start(ident[:, :], t["ident"]).then_inc(loaded_tok, 16)
            loads = ((iota8[:, :], t["iota8"]), (a0w[:, :, :], t["a0w"]), (rows1[:, :, :], t["rows1"]),
                     (cosT, t["cosT"]), (sinT, t["sinT"]), (mask0, t["mask0"]),
                     (pkwq[:, :], t["pkwq"]), (pkkeys[:, :], t["pkkeys"]),
                     (a1w[:, :, :], t["a1w"]), (wg[:, :], t["Wg"]),
                     (w1[:, :, :], t["W1"]), (w2[:, :, :], t["W2"]))
            assert len(loads) == N_LOADS
            for dst, src in loads:
                sp.dma_start(dst, src).then_inc(loaded_all, 16)

            def heads():
                for dram, chip in ((q_dram, QT), (k_dram, KT)):
                    for b in range(B):
                        sp.dma_start(dram[H * b:H * (b + 1)].rearrange("h d n -> (h d) n"),
                                     chip[:, T_PAD * b:T_PAD * (b + 1)]).then_inc(qk_stored, 16)
                sp.wait_ge(qk_stored, 32 * B)
                sp.sem_inc(qk_stored, -(32 * B))
                with sp.Fori(0, B * H // 2) as i:
                    for s in range(2):
                        sp.wait_ge(slot_free[s], 1)
                        sp.sem_inc(slot_free[s], -1)
                        n = i * 2 + s
                        sp.dma_start(q_slot[s][:, :], q_dram[bass.ds(n, 1), :, :].rearrange(
                            "a d n -> (a d) n")).then_inc(slot_loaded[s], 16)
                        sp.dma_start(k_slot[s][:, :], k_dram[bass.ds(n, 1), :, :].rearrange(
                            "a d n -> (a d) n")).then_inc(slot_loaded[s], 16)
                        sp.dma_start(v_slot[s][:, :, :], v_all[:, bass.ds(n, 1), :, :].rearrange(
                            "p a c w -> p (a c) w")).then_inc(slot_loaded[s], 16)

            if stop >= 1:
                enter_phase(sp, 3)
                heads()
            if stop >= 3:
                enter_phase(sp, 9)
                heads()
            enter_phase(sp, {0: 1, 1: 5, 2: 7, 3: 11}.get(stop, 13))
            for b in range(B):
                full = ROWS * (TPB - 1)
                sp.dma_start(t["out"][b, 0:full, :].rearrange("(i p) c -> p i c", p=ROWS),
                             h_tok[:, TPB * b:TPB * b + TPB - 1, :]).then_inc(stored, 16)
                sp.dma_start(t["out"][b, full:T_REAL, :],
                             h_tok[0:T_REAL - full, TPB * b + TPB - 1, :]).then_inc(stored, 16)
            sp.wait_ge(stored, 16 * 2 * B)
            sp.wait_ge(loaded_all, 16 * N_LOADS)

        @block.tensor
        def _(pe):
            def norm_transpose():
                for j in range(NT // 4):
                    pe.wait_ge(dve_ready, 1)
                    pe.sem_inc(dve_ready, -1)
                    for k in range(4):
                        ins = pe.transpose(bank[j][:, ROWS * k:ROWS * (k + 1)], xn_tok[:, 4 * j + k, :],
                                           ident[0:ROWS, 0:ROWS])
                    ins.then_inc(mm_ready, 1)

            def attention(layer):
                steps = HEADS_PER_BODY * TPB

                def n_chunks(i):
                    return chunks0[i] if layer == 0 else TPB

                def scores(n):
                    hd, i = divmod(n, TPB)
                    s = hd % 2
                    if i == 0:
                        pe.wait_ge(slot_loaded[s], 48)
                        pe.sem_inc(slot_loaded[s], -48)
                    lhsT = q_slot[s][:, ROWS * i:ROWS * (i + 1)]
                    if layer == 0:
                        w = ROWS * chunks0[i]
                        pe.matmul(bank[2 + n % 3][0:ROWS, 0:w], lhsT, k_slot[s][:, 0:w],
                                  start=True, stop=True).then_inc(s_ready, 1)
                    else:
                        pe.wait_ge(s_free, 1)
                        pe.sem_inc(s_free, -1)
                        b0 = 2 + 2 * (n % 2)
                        pe.matmul(bank[b0][0:ROWS, 0:512], lhsT, k_slot[s][:, 0:512], start=True, stop=True)
                        pe.matmul(bank[b0 + 1][0:ROWS, 0:T_REAL - 512], lhsT, k_slot[s][:, 512:T_REAL],
                                  start=True, stop=True).then_inc(s_ready, 1)

                def transposes(n):
                    pe.wait_ge(p_ready, 1)
                    pe.sem_inc(p_ready, -1)
                    for c in range(n_chunks(n % TPB)):
                        if layer == 0:
                            dst = bank[6 + n % 2][0:ROWS, ROWS * c:ROWS * (c + 1)]
                        else:
                            dst = bank[6 + c // 3][0:ROWS, ROWS * (c % 3):ROWS * (c % 3 + 1)]
                        ins = pe.transpose(dst, (pr0, pr1)[layer][n % 3][:, ROWS * c:ROWS * (c + 1)],
                                           ident[0:ROWS, 0:ROWS])
                    ins.then_inc(t_ready, 1)

                def values(n):
                    hd, i = divmod(n, TPB)
                    s = hd % 2
                    if i == 0:
                        pe.wait_ge(o_free[s], 1)
                        pe.sem_inc(o_free[s], -1)
                    pe.wait_ge(pt_ready, 1)
                    pe.sem_inc(pt_ready, -1)
                    for c in range(n_chunks(i)):
                        ins = pe.matmul(bank[s][0:ROWS, VW * i:VW * (i + 1)],
                                        (pt0, pt1)[layer][:, ROWS * c:ROWS * (c + 1)],
                                        v_slot[s][:, c, :], start=(c == 0), stop=(c == n_chunks(i) - 1))
                    if i == TPB - 1:
                        ins.then_inc(o_ready, 1)

                with pe.Fori(0, B * H // HEADS_PER_BODY):
                    scores(0)
                    scores(1)
                    for n in range(steps):
                        if n + 2 < steps:
                            scores(n + 2)
                        transposes(n)
                        values(n)
                end_phase(pe)

            def attention_out(w_o, b_row):
                def out_mm(j):
                    pe.wait_ge(act_ready_pe, 1)
                    pe.sem_inc(act_ready_pe, -1)
                    if j >= 2:
                        pe.wait_ge(dve_ready, 1)
                        pe.sem_inc(dve_ready, -1)
                    for k in range(4):
                        dst = bank[2 + j % 2][0:ROWS, C * k:C * (k + 1)]
                        pe.matmul(dst, oT[j % 2][:, ROWS * k:ROWS * (k + 1)], w_o, start=True, stop=False)
                        ins = pe.matmul(dst, ones_row[:, :], b_row, start=False, stop=True)
                    ins.then_inc(mm_ready_v, 1)

                for j in range(NT // 4):
                    for k in range(4):
                        b, i = divmod(4 * j + k, TPB)
                        ins = pe.transpose(bank[j % 2][:, ROWS * k:ROWS * (k + 1)],
                                           o_tok[:, b, i, :], ident[0:ROWS, 0:ROWS])
                    ins.then_inc(mm_ready, 1)
                    if j:
                        out_mm(j - 1)
                out_mm(NT // 4 - 1)
                end_phase(pe)

            pe.wait_ge(loaded_tok, 16 * 8)
            for j in range(2 * B):
                b, f = divmod(j, 2)
                pe.matmul(bank[j][:, 0:HALF], tokw[:, :], patches[:, b, HALF * f:HALF * (f + 1)],
                          start=True, stop=True).then_inc(mm_ready, 1)
            pe.wait_ge(dve_ready, 1)
            pe.sem_inc(dve_ready, -1)
            for j in range(NT // 4):
                for k in range(4):
                    n = 4 * j + k
                    ins = pe.transpose(bank[j][0:ROWS, C * k:C * (k + 1)], yT[:, ROWS * n:ROWS * (n + 1)],
                                       ident[:, :])
                ins.then_inc(mm_ready_v, 1)
            end_phase(pe)
            if stop < 1:
                return

            norm_transpose()
            end_phase(pe)
            pe.wait_ge(loaded_all, 16 * N_LOADS)
            for b in range(B):
                x_b = [xT[:, T_PAD * b + 375 * f:T_PAD * b + 375 * (f + 1)] for f in range(2)]
                if b:
                    pe.wait_ge(act_ready_pe, 1)
                    pe.sem_inc(act_ready_pe, -1)
                for w in range(2):
                    for f in range(2):
                        ins = pe.matmul(bank[2 * w + f][:, 0:375], a0w[:, w, :], x_b[f], start=True, stop=True)
                ins.then_inc(mm_ready_v, 1)
                if b:
                    pe.wait_ge(k_used, 1)
                    pe.sem_inc(k_used, -1)
                for w in range(2, 4):
                    for f in range(2):
                        ins = pe.matmul(bank[2 * w + f][:, 0:375], a0w[:, w, :], x_b[f], start=True, stop=True)
                ins.then_inc(mm_ready_v, 1)
                pe.wait_ge(q_used, 1)
                pe.sem_inc(q_used, -1)
                for c in range(4):
                    dst = bank[0][0:ROWS, C * c:C * (c + 1)]
                    pe.matmul(dst, xc[:, ROWS * c:ROWS * (c + 1)], a0w[:, 4, :], start=True, stop=False)
                    ins = pe.matmul(dst, ones_row[:, :], rows1[:, 0, :], start=False, stop=True)
                ins.then_inc(mm_ready, 1)
            pe.wait_ge(act_ready_pe, 1)
            pe.sem_inc(act_ready_pe, -1)
            pe.wait_ge(k_used, 1)
            pe.sem_inc(k_used, -1)
            end_phase(pe)
            attention(0)
            attention_out(a0w[:, 5, :], rows1[:, 1, :])
            if stop < 2:
                return
            norm_transpose()
            end_phase(pe)

            def pk_scores(n):
                for h in range(PK_HEADS):
                    ins = pe.matmul(bank[h // 4][:, ROWS * (h % 4):ROWS * (h % 4 + 1)],
                                    pkwq[:, C * h:C * (h + 1)], xT[:, bass.ds(n * ROWS, ROWS)],
                                    start=True, stop=True)
                ins.then_inc(mm_ready, 1)
                pe.wait_ge(act_ready_pe, 1)
                pe.sem_inc(act_ready_pe, -1)
                pe.wait_ge(scores_free, 1)
                pe.sem_inc(scores_free, -1)
                for c in range(2):
                    for h in range(PK_HEADS):
                        ins = pe.matmul(bank[2 + 2 * c + h // 4][0:ROWS, C * (h % 4):C * (h % 4 + 1)],
                                        qhT[64 * c:64 * (c + 1), h, :], pkkeys[64 * c:64 * (c + 1), C * h:C * (h + 1)],
                                        start=True, stop=True)
                ins.then_inc(scores_ready, 1)

            def pk_sum():
                pe.wait_ge(usum_free, 1)
                pe.sem_inc(usum_free, -1)
                for c in range(4):
                    pe.wait_ge(up_ready, 1)
                    pe.sem_inc(up_ready, -1)
                    for r in range(RING // 4):
                        ins = pe.matmul(bank[6][0:ROWS, :], ident[0:ROWS, 0:ROWS],
                                        G[0:ROWS, c, 4 * r:4 * r + 4, C:2 * C],
                                        start=(c == 0 and r == 0), stop=(c == 3 and r == RING // 4 - 1))
                    ins.then_inc(ring_free[c] if c < 3 else usum_ready, 1)

            pk_scores(0)
            with pe.Fori(0, NT - 1) as n:
                pk_scores(n + 1)
                pk_sum()
            pk_sum()
            end_phase(pe)
            if stop < 3:
                return
            norm_transpose()
            end_phase(pe)
            pe.wait_ge(dve_ready, 1)
            pe.sem_inc(dve_ready, -1)
            for b in range(B):
                if b:
                    pe.wait_ge(act_ready_pe, 1)
                    pe.sem_inc(act_ready_pe, -1)
                for w in range(2):
                    for f in range(2):
                        ins = pe.matmul(bank[2 * w + f][:, 0:375], a1w[:, w, :],
                                        conv_x[:, T_PAD * b + 375 * f:T_PAD * b + 375 * (f + 1)],
                                        start=True, stop=True)
                ins.then_inc(mm_ready, 1)
                if b:
                    pe.wait_ge(dve_ready, 1)
                    pe.sem_inc(dve_ready, -1)
                for c in range(TPB):
                    dst = bank[4 + c // 3][0:ROWS, C * (c % 3):C * (c % 3 + 1)]
                    at = T_PAD * b + ROWS * c
                    pe.matmul(dst, conv_x[:, at:at + ROWS], a1w[:, 2, :], start=True, stop=False)
                    ins = pe.matmul(dst, ones_row[:, :], rows1[:, 2, :], start=False, stop=True)
                ins.then_inc(mm_ready_v, 1)
            pe.wait_ge(act_ready_pe, 1)
            pe.sem_inc(act_ready_pe, -1)
            pe.wait_ge(dve_ready, 1)
            pe.sem_inc(dve_ready, -1)
            end_phase(pe)
            attention(1)
            attention_out(a1w[:, 3, :], rows1[:, 3, :])
            if stop < 4:
                return
            norm_transpose()
            for j in range(NT // 4):
                pe.wait_ge(act_ready_pe, 1)
                pe.sem_inc(act_ready_pe, -1)
                for k in range(4):
                    n = 4 * j + k
                    ins = pe.matmul(bank[7][0:ROWS, EXPERTS * n:EXPERTS * (n + 1)],
                                    xT[:, ROWS * n:ROWS * (n + 1)], wg[:, :], start=True, stop=True)
            ins.then_inc(mm_ready_v, 1)
            for j in range(NT // 4):
                for i in range(2):
                    pe.wait_ge(dve_ready, 1)
                    pe.sem_inc(dve_ready, -1)
                    for k in range(4):
                        ins = pe.transpose(bank[2 * (j % 2) + i][:, ROWS * k:ROWS * (k + 1)],
                                           xs[:, j % 2, i, k, :], ident[0:ROWS, 0:ROWS])
                    ins.then_inc(mm_ready, 1)
            end_phase(pe)

            with pe.Fori(0, TOK // GROUP) as g:
                def hidden(m):
                    for i in range(2):
                        pe.matmul(bank[2 * (m % 2) + i][:, 0:GROUP], w1[:, m, :],
                                  wT[i][:, bass.ds(g * GROUP, GROUP)], start=True, stop=True).then_inc(z_ready, 1)

                hidden(0)
                hidden(1)
                for m in range(FCH):
                    pe.wait_ge(gs_ready, 1)
                    pe.sem_inc(gs_ready, -1)
                    ins = pe.matmul(bank[4][:, 0:GROUP], w2[:, m, :], g_sum[m % 2],
                                    start=(m == 0), stop=(m == FCH - 1))
                    if m == FCH - 1:
                        ins.then_inc(mm_ready_v, 1)
                    if m + 2 < FCH:
                        hidden(m + 2)
                pe.wait_ge(dve_ready, 1)
                pe.sem_inc(dve_ready, -1)
                for k in range(4):
                    ins = pe.transpose(bank[5][0:ROWS, C * k:C * (k + 1)], yT_ffn[:, ROWS * k:ROWS * (k + 1)],
                                       ident[:, :])
                ins.then_inc(mm_ready_v, 1)
            end_phase(pe)

        @block.scalar
        def _(act):
            def norm_part(signal=None):
                act.wait_ge(dve_to_act, 1)
                act.sem_inc(dve_to_act, -1)
                act.activation(std[0:ROWS, :], std[0:ROWS, :], ACT.Sqrt).then_inc(act_ready, 1)
                for j in range(NT // 4):
                    act.wait_ge(mm_ready, 1)
                    act.sem_inc(mm_ready, -1)
                    ins = act.copy(xT[:, GROUP * j:GROUP * (j + 1)], bank[j][:, 0:GROUP])
                    if signal is not None:
                        ins.then_inc(signal, 1)

            def attention0():
                with act.Fori(0, B * H // HEADS_PER_BODY):
                    for n in range(HEADS_PER_BODY * TPB):
                        w = ROWS * chunks0[n % TPB]
                        act.wait_ge(s_masked, 1)
                        act.sem_inc(s_masked, -1)
                        act.activation(pr0[n % 3][:, 0:w], sm0[n % 3][:, 0:w], ACT.Exp,
                                       bias=negmax[:, n % 3:n % 3 + 1], scale=-1.0).then_inc(p_ready, 1)
                        act.wait_ge(t_ready, 1)
                        act.sem_inc(t_ready, -1)
                        act.copy(pt0[:, 0:w], bank[6 + n % 2][0:ROWS, 0:w]).then_inc(pt_ready, 1)
                end_phase(act)

            def attention1():
                act.sem_inc(s_free, 2)
                pt_psum = psum[0:ROWS, 4 * 512:6 * 512].rearrange("p (a n) -> p a n", a=2)[:, :, 0:375]

                def exp_all(n):
                    act.wait_ge(s_replaced[0], 1)
                    act.sem_inc(s_replaced[0], -1)
                    at = 1024 * (n % 2)
                    act.activation(e_a[n % 3][:, 0:T_REAL], psum[0:ROWS, at:at + T_REAL], ACT.Exp,
                                   bias=negmax[:, n % 3:n % 3 + 1], scale=SCALE1).then_inc(s_free, 1)

                def exp_rest(n):
                    act.wait_ge(s_replaced[1], 1)
                    act.sem_inc(s_replaced[1], -1)
                    act.activation(w_b[n % 3][:, 0:T_REAL], w_b[n % 3][:, 0:T_REAL], ACT.Exp,
                                   bias=negmax[:, n % 3:n % 3 + 1], scale=SCALE1).then_inc(e_ready, 1)

                def move(n):
                    act.wait_ge(t_ready, 1)
                    act.sem_inc(t_ready, -1)
                    act.copy(pt1.rearrange("p (a n) -> p a n", a=2), pt_psum).then_inc(pt_ready, 1)

                steps = HEADS_PER_BODY * TPB
                with act.Fori(0, B * H // HEADS_PER_BODY):
                    for n in range(steps):
                        if n:
                            exp_rest(n - 1)
                        exp_all(n)
                        if n:
                            move(n - 1)
                    exp_rest(steps - 1)
                    move(steps - 1)
                end_phase(act)

            def attention_out():
                for j in range(NT // 4):
                    act.wait_ge(mm_ready, 1)
                    act.sem_inc(mm_ready, -1)
                    act.copy(oT[j % 2], bank[j % 2][:, 0:GROUP]).then_inc(act_ready_pe, 1)
                end_phase(act)

            act.wait_ge(loaded_tok, 16 * 8)
            for j in range(2 * B):
                b, f = divmod(j, 2)
                at = T_PAD * b + HALF * f
                act.wait_ge(mm_ready, 1)
                act.sem_inc(mm_ready, -1)
                act.activation(yT[:, at:at + HALF], bank[j][:, 0:HALF], ACT.Relu,
                               bias=col("tok_b")).then_inc(act_ready, 1)
            act.wait_ge(dve_to_act, 1)
            act.sem_inc(dve_to_act, -1)
            act.activation(bn[:, 2:3], bn[:, 2:3], ACT.Sqrt).then_inc(act_ready, 1)
            end_phase(act)
            if stop < 1:
                return
            norm_part()
            end_phase(act)
            for b in range(B):
                act.wait_ge(mm_ready, 1)
                act.sem_inc(mm_ready, -1)
                act.copy(v_all[:, H * b:H * (b + 1), 0:4, 0:DH].rearrange("p h c d -> p c h d"),
                         bank[0][0:ROWS, :].rearrange("p (c h d) -> p c h d", c=4, h=H)).then_inc(act_ready_pe, 1)
            end_phase(act)
            attention0()
            attention_out()
            if stop < 2:
                return
            norm_part()
            end_phase(act)

            def pk_queries():
                act.wait_ge(mm_ready, 1)
                act.sem_inc(mm_ready, -1)
                for h in range(PK_HEADS):
                    ins = act.activation(qhT[:, h, :], bank[h // 4][:, ROWS * (h % 4):ROWS * (h % 4 + 1)],
                                         ACT.Identity, bias=col("pkbq", h))
                ins.then_inc(act_ready_pe, 1)
                act.wait_ge(dve_to_act, 1)
                act.sem_inc(dve_to_act, -1)
                act.activation(w_next[:, :, :], w_next[:, :, :], ACT.Exp).then_inc(act_ready, 1)

            def pk_tanh():
                for k in range(2):
                    act.wait_ge(dve_to_act, 1)
                    act.sem_inc(dve_to_act, -1)
                    act.activation(gl[:, 2, :], gl[:, 0, :], ACT.Tanh, scale=GELU_A).then_inc(act_ready, 1)

            pk_queries()
            with act.Fori(0, NT - 1):
                pk_queries()
                pk_tanh()
            pk_tanh()
            end_phase(act)
            if stop < 3:
                return
            norm_part()
            end_phase(act)
            for b in range(B):
                act.wait_ge(mm_ready, 1)
                act.sem_inc(mm_ready, -1)
                for w, (dst, bias) in enumerate(((QT, col("l1q")), (KT, col("l1k")))):
                    for f in range(2):
                        at = T_PAD * b + 375 * f
                        ins = act.activation(dst[:, at:at + 375], bank[2 * w + f][:, 0:375],
                                             ACT.Identity, bias=bias)
                ins.then_inc(act_ready_pe, 1)
            end_phase(act)
            attention1()
            attention_out()
            if stop < 4:
                return
            norm_part(act_ready_pe)
            act.wait_ge(dve_to_act, 1)
            act.sem_inc(dve_to_act, -1)
            act.activation(lg[:, :, :], lg[:, :, :], ACT.Exp).then_inc(act_ready, 1)
            for j in range(NT // 4):
                for i in range(2):
                    act.wait_ge(mm_ready, 1)
                    act.sem_inc(mm_ready, -1)
                    act.copy(wT[i][:, GROUP * j:GROUP * (j + 1)],
                             bank[2 * (j % 2) + i][:, 0:GROUP]).then_inc(act_ready, 1)
            end_phase(act)
            with act.Fori(0, TOK // GROUP):
                for m in range(FCH):
                    for i in range(2):
                        act.wait_ge(z_ready, 1)
                        act.sem_inc(z_ready, -1)
                        act.activation(g_act[m % 2][i], bank[2 * (m % 2) + i][:, 0:GROUP], ACT.Gelu,
                                       bias=col("b1", m)).then_inc(g_ready, 1)
            end_phase(act)

        @block.vector
        def _(dve):
            def settle(ins):
                ins.then_inc(dve_self, 1)
                dve.wait_ge(dve_self, 1)
                dve.sem_inc(dve_self, -1)

            def norm_part():
                for n in range(NT):
                    ins = dve.bn_stats(stats[0:ROWS, n, :], h_tok[:, n, :])
                settle(ins)
                for n in range(NT):
                    ins = dve.bn_aggr(mv[0:ROWS, n, :], stats[0:ROWS, n, :])
                settle(ins)
                dve.tensor_scalar(std[0:ROWS, :], mv[0:ROWS, :, 1], EPS, None, ALU.add).then_inc(dve_to_act, 1)
                dve.wait_ge(act_ready, 1)
                dve.sem_inc(act_ready, -1)
                settle(dve.reciprocal(rstd[0:ROWS, :], std[0:ROWS, :]))
                for n in range(NT):
                    ins = dve.tensor_scalar(xn_tok[:, n, :], h_tok[:, n, :], mv[0:ROWS, n, 0:1],
                                            rstd[0:ROWS, n:n + 1], ALU.subtract, ALU.mult)
                    if n % 4 == 3:
                        ins.then_inc(dve_ready, 1)

            def attention(layer):
                steps = HEADS_PER_BODY * TPB
                if layer == 0:
                    for s in range(2):
                        dve.sem_inc(o_free[s], 1)
                        dve.sem_inc(slot_free[s], 1)

                def mask_and_max(n):
                    i = n % TPB
                    w = ROWS * chunks0[i]
                    dve.wait_ge(s_ready, 1)
                    dve.sem_inc(s_ready, -1)
                    dve.tensor_tensor_reduce(sm0[n % 3][:, 0:w], bank[2 + n % 3][0:ROWS, 0:w], mask0[:, i, 0:w],
                                             -SCALE0, -NEG, ALU.add, ALU.min,
                                             negmax[:, n % 3:n % 3 + 1]).then_inc(s_masked, 1)

                def top16(n):
                    at = 1024 * (n % 2)
                    s_n = psum[0:ROWS, at:at + T_REAL]
                    top = m16[:, n % 3, :]
                    dve.wait_ge(s_ready, 1)
                    dve.sem_inc(s_ready, -1)
                    settle(dve.max(top[:, 0:8], s_n))
                    dve.match_replace(w_a[:, 0:T_REAL], top[:, 0:8], s_n, NEG).then_inc(dve_self, 1)
                    dve.tensor_scalar(negmax[:, n % 3:n % 3 + 1], top[:, 0:1], -SCALE1, None,
                                      ALU.mult).then_inc(s_replaced[0], 1)
                    dve.wait_ge(dve_self, 1)
                    dve.sem_inc(dve_self, -1)
                    settle(dve.max(top[:, 8:16], w_a[:, 0:T_REAL]))
                    dve.match_replace(w_b[n % 3][:, 0:T_REAL], top[:, 8:16], w_a[:, 0:T_REAL],
                                      NEG).then_inc(s_replaced[1], 1)

                def head_out(b, quad, hd):
                    s = hd % 2
                    o = bank[s][0:ROWS, 0:TPB * VW].rearrange("p (i w) -> p i w", i=TPB)
                    dve.wait_ge(o_ready, 1)
                    dve.sem_inc(o_ready, -1)
                    dve.sem_inc(slot_free[s], 1)
                    settle(dve.reciprocal(recip[:, s, :], o[:, :, DH]))
                    dve.tensor_tensor(
                        o_tok[:, bass.ds(b, 1), :, bass.ds(quad * (HEADS_PER_BODY * DH) + hd * DH, DH)].rearrange(
                            "p a i d -> p (a i) d"),
                        o[:, :, 0:DH], recip[:, s, :].unsqueeze(2).to_broadcast([ROWS, TPB, DH]),
                        ALU.mult).then_inc(o_free[s], 1)

                with dve.Fori(0, B) as b, dve.Fori(0, H // HEADS_PER_BODY) as quad:
                    for n in range(steps):
                        (mask_and_max, top16)[layer](n)
                        if n > TPB and n % TPB == 2:
                            head_out(b, quad, n // TPB - 1)
                    head_out(b, quad, HEADS_PER_BODY - 1)
                end_phase(dve)

            def attention_out():
                for j in range(NT // 4):
                    dve.wait_ge(mm_ready_v, 1)
                    dve.sem_inc(mm_ready_v, -1)
                    hj = h_tok[:, 4 * j:4 * j + 4, :]
                    dve.tensor_tensor(hj, hj, bank[2 + j % 2][0:ROWS, :].rearrange("p (k c) -> p k c", k=4),
                                      ALU.add).then_inc(dve_ready, 1)
                dve.wait_ge(dve_ready, 2)
                dve.sem_inc(dve_ready, -2)
                end_phase(dve)

            dve.memset(yT.rearrange("p (b n) -> p b n", b=B)[:, :, T_REAL:T_PAD], 0.0)
            dve.memset(ones_row[:, :], 1.0)
            for j in range(2 * B):
                b, f = divmod(j, 2)
                at = T_PAD * b + HALF * f
                dve.wait_ge(act_ready, 1)
                dve.sem_inc(act_ready, -1)
                ins = dve.bn_stats(stats[:, j, :], yT[:, at:at + HALF])
            dve.wait_ge(loaded_tok, 16 * 8)
            settle(ins)
            settle(dve.bn_aggr(bn[:, 0:2], stats[:, 0:2 * B, :].rearrange("p j s -> p (j s)")))
            dve.tensor_scalar(bn[:, 2:3], bn[:, 1:2], EPS, None, ALU.add).then_inc(dve_to_act, 1)
            dve.wait_ge(act_ready, 1)
            dve.sem_inc(act_ready, -1)
            settle(dve.reciprocal(bn[:, 3:4], bn[:, 2:3]))
            settle(dve.tensor_tensor(bn[:, 4:5], bn[:, 3:4], col("gamma"), ALU.mult))
            settle(dve.tensor_tensor(bn[:, 5:6], bn[:, 0:1], bn[:, 4:5], ALU.mult))
            settle(dve.tensor_tensor(bn[:, 6:7], col("beta"), bn[:, 5:6], ALU.subtract))
            dve.tensor_scalar(yT, yT, bn[:, 4:5], bn[:, 6:7], ALU.mult, ALU.add).then_inc(dve_ready, 1)
            for j in range(NT // 4):
                dve.wait_ge(mm_ready_v, 1)
                dve.sem_inc(mm_ready_v, -1)
                dve.tensor_copy(h_tok[:, 4 * j:4 * j + 4, :], bank[j][0:ROWS, :].rearrange("p (k c) -> p k c", k=4))
            end_phase(dve)
            if stop < 1:
                return
            norm_part()
            end_phase(dve)
            dve.wait_ge(loaded_all, 16 * N_LOADS)
            settle(dve.memset(KT, 0.0))
            settle(dve.memset(xc[:, KEYS0:KEYS0_PAD], 0.0))

            def rotate(bk, rot_a, rot_b, bias, bias_sw):
                for f in range(2):
                    half = slice(375 * f, 375 * (f + 1))
                    dve.scalar_tensor_tensor(rot_a[:, half], bank[bk + f][:, 0:375], bias, cosT[:, half],
                                             ALU.add, ALU.mult)
                    ins = dve.scalar_tensor_tensor(rot_b[:, half], bank[bk + 2 + f][:, 0:375], bias_sw,
                                                   sinT[:, half], ALU.add, ALU.mult)
                settle(ins)

            def seen(a):
                return a[:, 2:2 + 3 * PAIRS0].rearrange("p (g r) -> p g r", r=3)[:, :, 0:2]

            def packed(a):
                return a[:, 2:KEYS0].rearrange("p (g r) -> p g r", r=2)

            for b in range(B):
                x_b = xT[:, T_PAD * b:T_PAD * (b + 1)]
                k_b = KT[:, T_PAD * b:T_PAD * (b + 1)]
                dve.wait_ge(mm_ready_v, 1)
                dve.sem_inc(mm_ready_v, -1)
                dve.tensor_copy(xc[:, 0:2], x_b[:, 0:2])
                dve.tensor_copy(packed(xc), seen(x_b))
                rotate(0, *rot_q, col("bq"), col("bqs"))
                dve.tensor_tensor(QT[:, T_PAD * b:T_PAD * (b + 1)], *rot_q, ALU.add).then_inc(q_used, 1)
                dve.wait_ge(mm_ready_v, 1)
                dve.sem_inc(mm_ready_v, -1)
                rotate(4, *rot_k, col("bk"), col("bks"))
                dve.tensor_tensor(k_b[:, 0:2], rot_k[0][:, 0:2], rot_k[1][:, 0:2], ALU.add)
                dve.tensor_tensor(packed(k_b), seen(rot_k[0]), seen(rot_k[1]), ALU.add).then_inc(k_used, 1)
            end_phase(dve)
            attention(0)
            attention_out()
            if stop < 2:
                return
            norm_part()
            end_phase(dve)

            def score(c, h):
                return bank[2 + 2 * c + h // 4][0:ROWS, C * (h % 4):C * (h % 4 + 1)]

            def pk_rank(parity):
                dve.wait_ge(scores_ready, 1)
                dve.sem_inc(scores_ready, -1)
                for c in range(2):
                    for h in range(PK_HEADS):
                        ins = dve.max(s8[:, c, h, :], score(c, h))
                settle(ins)
                for c in range(2):
                    for h in range(PK_HEADS):
                        ins = dve.max_index(i8[:, c, h, :], s8[:, c, h, :], score(c, h))
                ins.then_inc(scores_free, 1)
                settle(dve.tensor_tensor(
                    pair_s[:, :, :].rearrange("p h (i j) -> p h i j", i=8),
                    s8[:, 0, :, :].unsqueeze(3).to_broadcast([ROWS, H, 8, 8]),
                    s8[:, 1, :, :].unsqueeze(2).to_broadcast([ROWS, H, 8, 8]), ALU.add))
                dve.tensor_copy(i8f[:, :, :, :], i8[:, :, :, :])
                for h in range(PK_HEADS):
                    ins = dve.max(best[:, h, :], pair_s[:, h, :])
                settle(ins)
                for h in range(PK_HEADS):
                    ins = dve.max_index(pos[:, h, :], best[:, h, :], pair_s[:, h, :])
                settle(ins)
                flat = pos[:, :, :].rearrange("p h k -> p (h k)")
                dve.tensor_scalar(pos_ij[:, 0, :], flat, 3, None, ALU.logical_shift_right)
                dve.tensor_scalar(pos_ij[:, 1, :], flat, 7, None, ALU.bitwise_and).then_inc(dve_self, 1)
                dve.tensor_tensor(w_next[:, :, :], best[:, :, :], best[:, :, 0:1].to_broadcast([ROWS, H, 8]),
                                  ALU.subtract).then_inc(dve_to_act, 1)
                dve.wait_ge(dve_self, 1)
                dve.sem_inc(dve_self, -1)
                for c in range(2):
                    ins = dve.tensor_tensor(onehot[:, c, :, :],
                                            iota8[0:ROWS, :].unsqueeze(1).to_broadcast([ROWS, 64, 8]),
                                            pos_ij[:, c, :].unsqueeze(2).to_broadcast([ROWS, 64, 8]), ALU.is_equal)
                settle(ins)
                for c in range(2):
                    oh = onehot[:, c, :, :].rearrange("p (h k) i -> p h k i", h=H)
                    ins = dve.tensor_tensor(oh, oh, i8f[:, c, :, :].unsqueeze(2).to_broadcast([ROWS, H, 8, 8]),
                                            ALU.mult)
                settle(ins)
                settle(dve.tensor_reduce(r_ij[:, :, :], onehot[:, :, :, :], AX.X, ALU.add))
                dve.scalar_tensor_tensor(idx[parity][0:ROWS, :], r_ij[:, 0, :], float(C), r_ij[:, 1, :],
                                         ALU.mult, ALU.add).then_inc(idx_ready, 1)
                dve.wait_ge(act_ready, 1)
                dve.sem_inc(act_ready, -1)
                settle(dve.tensor_reduce(pk8[:, :], w_next[:, :, :], AX.X, ALU.add))
                settle(dve.reciprocal(pk8[:, :], pk8[:, :]))
                settle(dve.tensor_tensor(w_next[:, :, :], w_next[:, :, :],
                                         pk8[:, :].unsqueeze(2).to_broadcast([ROWS, H, 8]), ALU.mult))

            def pk_keep(n):
                dve.tensor_copy(w_cur[:, :], w_next[:, :, :].rearrange("p h k -> p (h k)"))
                settle(dve.tensor_copy(q_cur[:, :], xn_tok[:, bass.ds(n, 1), :].rearrange("p a c -> p (a c)")))

            def pk_mix(n):
                for k in range(2):
                    for c in (2 * k, 2 * k + 1):
                        dve.wait_ge(gathered[c], n * 256 + 256)
                        down = G[0:ROWS, c, :, 0:C]
                        settle(dve.tensor_tensor(down, down, q_cur[:, :].unsqueeze(1).to_broadcast([ROWS, RING, C]),
                                                 ALU.mult))
                        ins = dve.tensor_reduce(xdot[:, RING * c:RING * (c + 1)], down, AX.X, ALU.add)
                    settle(ins)
                    x = xdot[:, 2 * RING * k:2 * RING * (k + 1)]
                    settle(dve.tensor_tensor(gl[:, 0, :], x, x, ALU.mult))
                    settle(dve.tensor_scalar(gl[:, 1, :], gl[:, 0, :], GELU_B, 1.0, ALU.mult, ALU.add))
                    dve.tensor_tensor(gl[:, 0, :], gl[:, 1, :], x, ALU.mult).then_inc(dve_to_act, 1)
                    dve.wait_ge(act_ready, 1)
                    dve.sem_inc(act_ready, -1)
                    settle(dve.scalar_tensor_tensor(gl[:, 1, :], gl[:, 2, :], 1.0, x, ALU.add, ALU.mult))
                    v = vals[:, 2 * RING * k:2 * RING * (k + 1)]
                    settle(dve.scalar_tensor_tensor(v, gl[:, 1, :], 0.5, w_cur[:, 2 * RING * k:2 * RING * (k + 1)],
                                                    ALU.mult, ALU.mult))
                    for c in (2 * k, 2 * k + 1):
                        up = G[0:ROWS, c, :, C:2 * C]
                        dve.tensor_tensor(up, up, vals[:, RING * c:RING * (c + 1)].unsqueeze(2).to_broadcast(
                            [ROWS, RING, C]), ALU.mult).then_inc(up_ready, 1)
                dve.wait_ge(usum_ready, 1)
                dve.sem_inc(usum_ready, -1)
                dve.sem_inc(ring_free[3], 1)
                settle(dve.tensor_reduce(usum[:, :], bank[6][0:ROWS, :].rearrange("p (r c) -> p c r", r=4),
                                         AX.X, ALU.add))
                h_n = h_tok[:, bass.ds(n, 1), :].rearrange("p a c -> p (a c)")
                dve.tensor_tensor(h_n, h_n, usum[:, :], ALU.add).then_inc(usum_free, 1)

            dve.sem_inc(scores_free, 1)
            dve.sem_inc(usum_free, 1)
            for p in range(2):
                ins = dve.memset(idx[p][:, :], 0)
            settle(ins)
            pk_rank(0)
            with dve.Fori(0, NT // 2 - 1) as pair:
                for p in range(2):
                    pk_keep(pair * 2 + p)
                    pk_rank(1 - p)
                    pk_mix(pair * 2 + p)
            pk_keep(NT - 2)
            pk_rank(1)
            pk_mix(NT - 2)
            pk_keep(NT - 1)
            pk_mix(NT - 1)
            end_phase(dve)
            if stop < 3:
                return
            norm_part()
            end_phase(dve)
            x4, c4 = (a.rearrange("p (b n) -> p b n", b=B) for a in (xT[:, :], conv_t))
            settle(dve.tensor_scalar(conv_t, xT[:, :], col("conv", 1), col("conv_b"), ALU.mult, ALU.add))
            settle(dve.scalar_tensor_tensor(c4[:, :, 1:T_REAL], x4[:, :, 0:T_REAL - 1], col("conv", 0),
                                            c4[:, :, 1:T_REAL], ALU.mult, ALU.add))
            settle(dve.scalar_tensor_tensor(c4[:, :, 0:T_REAL - 1], x4[:, :, 1:T_REAL], col("conv", 2),
                                            c4[:, :, 0:T_REAL - 1], ALU.mult, ALU.add))
            dve.tensor_tensor(conv_x, xT[:, :], conv_t, ALU.add).then_inc(dve_ready, 1)
            for b in range(B):
                dve.wait_ge(mm_ready_v, 1)
                dve.sem_inc(mm_ready_v, -1)
                for f in range(2):
                    ins = dve.tensor_copy(
                        v_all[:, H * b:H * (b + 1), 3 * f:3 * f + 3, 0:DH].rearrange("p h c d -> p c h d"),
                        bank[4 + f][0:ROWS, 0:3 * C].rearrange("p (c h d) -> p c h d", c=3, h=H))
                ins.then_inc(dve_ready, 1)
            end_phase(dve)
            attention(1)
            attention_out()
            if stop < 4:
                return
            norm_part()
            dve.wait_ge(mm_ready_v, 1)
            dve.sem_inc(mm_ready_v, -1)
            logits = bank[7][0:ROWS, 0:NT * EXPERTS].rearrange("p (n e) -> p n e", e=EXPERTS)
            full = [ROWS, NT, EXPERTS]
            settle(dve.tensor_reduce(lg_m[:, :], logits, AX.X, ALU.max))
            dve.tensor_tensor(lg[:, :, :], logits, lg_m[:, :].unsqueeze(2).to_broadcast(full),
                              ALU.subtract).then_inc(dve_to_act, 1)
            dve.wait_ge(act_ready, 1)
            dve.sem_inc(act_ready, -1)
            settle(dve.tensor_reduce(lg_m[:, :], lg[:, :, :], AX.X, ALU.add))
            settle(dve.reciprocal(lg_m[:, :], lg_m[:, :]))
            settle(dve.tensor_tensor(lg[:, :, :], lg[:, :, :], lg_m[:, :].unsqueeze(2).to_broadcast(full), ALU.mult))
            for n in range(NT):
                ins = dve.max(top_p[:, n, :], lg[:, n, :])
            settle(ins)
            settle(dve.tensor_tensor(lg_m[:, :], top_p[:, :, 0], top_p[:, :, 1], ALU.add))
            settle(dve.reciprocal(lg_m[:, :], lg_m[:, :]))
            for i in range(2):
                ins = dve.tensor_tensor(p_i[:, i, :], top_p[:, :, i], lg_m[:, :], ALU.mult)
            settle(ins)
            for j in range(NT // 4):
                if j >= 2:
                    dve.wait_ge(act_ready, 2)
                    dve.sem_inc(act_ready, -2)
                for i in range(2):
                    dve.tensor_tensor(xs[:, j % 2, i, :, :], xn_tok[:, 4 * j:4 * j + 4, :],
                                      p_i[:, i, 4 * j:4 * j + 4].unsqueeze(2).to_broadcast([ROWS, 4, C]),
                                      ALU.mult).then_inc(dve_ready, 1)
            dve.wait_ge(act_ready, 4)
            dve.sem_inc(act_ready, -4)
            settle(dve.tensor_reduce(bn[:, 6:7], cols[:, COL["b2"]:COL["b2"] + EXPERTS], AX.X, ALU.add))
            dve.tensor_scalar(bn[:, 7:8], bn[:, 6:7], 2.0, None, ALU.mult)
            end_phase(dve)
            with dve.Fori(0, TOK // GROUP) as g:
                for m in range(FCH):
                    dve.wait_ge(g_ready, 2)
                    dve.sem_inc(g_ready, -2)
                    dve.tensor_tensor(g_sum[m % 2], g_act[m % 2][0], g_act[m % 2][1], ALU.add).then_inc(gs_ready, 1)
                dve.wait_ge(mm_ready_v, 1)
                dve.sem_inc(mm_ready_v, -1)
                dve.tensor_scalar(yT_ffn, bank[4][:, 0:GROUP], bn[:, 7:8], None, ALU.add).then_inc(dve_ready, 1)
                dve.wait_ge(mm_ready_v, 1)
                dve.sem_inc(mm_ready_v, -1)
                h_g = h_tok[:, bass.ds(g * 4, 4), :]
                dve.tensor_tensor(h_g, h_g, bank[5][0:ROWS, :].rearrange("p (k c) -> p k c", k=4), ALU.add)
            end_phase(dve)

        @block.gpsimd
        def _(pool):
            pool.memset(v_all[:, :, :, :], 1.0)
            end_phase(pool)
            if stop < 1:
                return
            end_phase(pool)
            end_phase(pool)
            end_phase(pool)
            end_phase(pool)
            if stop < 2:
                return
            end_phase(pool)
            for c in range(4):
                pool.sem_inc(ring_free[c], 1)
            with pool.Fori(0, NT // 2):
                for p in range(2):
                    pool.wait_ge(idx_ready, 1)
                    pool.sem_inc(idx_ready, -1)
                    for c in range(4):
                        pool.wait_ge(ring_free[c], 1)
                        pool.sem_inc(ring_free[c], -1)
                        for r in range(RING):
                            k = RING * c + r
                            pool.indirect_dma_start(
                                out=G[:, c, r, :], out_offset=None, in_=t["tables"],
                                in_offset=bass.IndirectOffsetOnAxis(ap=idx[p][:, k:k + 1], axis=0),
                            ).then_inc(gathered[c], 16)
            end_phase(pool)
            if stop < 3:
                return
            end_phase(pool)
            end_phase(pool)
            for k in range(3):
                ins = pool.memset(pr1[k][:, T_REAL:T_PAD], 0.0)
            ins.then_inc(pool_self, 1)
            pool.wait_ge(pool_self, 1)
            pool.sem_inc(pool_self, -1)
            with pool.Fori(0, B * H // HEADS_PER_BODY):
                for n in range(HEADS_PER_BODY * TPB):
                    pool.wait_ge(e_ready, 1)
                    pool.sem_inc(e_ready, -1)
                    pool.tensor_tensor(pr1[n % 3][:, 0:T_REAL], e_a[n % 3][:, 0:T_REAL],
                                       w_b[n % 3][:, 0:T_REAL], ALU.subtract).then_inc(p_ready, 1)
            end_phase(pool)
            end_phase(pool)
            if stop < 4:
                return
            end_phase(pool)
            end_phase(pool)


def layouts(inputs):
    import numpy as np
    a = {k: np.asarray(v) for k, v in inputs.items()}
    swap = np.arange(C).reshape(-1, 2)[:, ::-1].reshape(-1)
    d = {}
    d["x"] = a["x"].transpose(2, 0, 1)
    d["tok_W"] = a["L0_tok_W"].T
    d["cols"] = np.concatenate(
        [a["L0_tok_b"][:, None], a["L0_tok_gamma"][:, None], a["L0_tok_beta"][:, None],
         a["L0_attn_bq"][:, None], a["L0_attn_bq"][swap][:, None],
         a["L0_attn_bk"][:, None], a["L0_attn_bk"][swap][:, None],
         a["L1_attn_conv_w"][:, 0, :], a["L1_attn_conv_b"][:, None],
         a["L1_attn_b_qkv"][0:C][:, None], a["L1_attn_b_qkv"][C:2 * C][:, None],
         a["L0_ffn_bq"].reshape(PK_HEADS, C).T, a["L1_ffn_b1"].reshape(FCH, C).T,
         a["L1_ffn_b2"].T, a["L1_ffn_b2"].T[:, 0:3]], axis=1)
    d["ident"] = np.eye(C, dtype=np.float32)
    d["iota8"] = np.broadcast_to(np.arange(PK_TOP, dtype=np.float32), (C, PK_TOP))
    d["a0w"] = np.stack([a["L0_attn_Wq"], a["L0_attn_Wq"][:, swap], a["L0_attn_Wk"], a["L0_attn_Wk"][:, swap],
                         a["L0_attn_Wv"], a["L0_attn_Wo"]], axis=1)
    d["rows1"] = np.stack([a["L0_attn_bv"], a["L0_attn_bo"], a["L1_attn_b_qkv"][2 * C:], a["L1_attn_b_o"]])[None]
    inv_freq = (np.float32(1.0) / np.float32(10000.0) ** (np.arange(0, C, 2, dtype=np.float32) / np.float32(C)))
    ang = np.repeat(inv_freq.astype(np.float32)[:, None] * np.arange(T_PAD, dtype=np.float32)[None, :], 2, axis=0)
    sign = np.where(np.arange(C) % 2 == 0, -1.0, 1.0).astype(np.float32)[:, None]
    d["cosT"] = np.cos(ang).astype(np.float32)
    d["sinT"] = (np.sin(ang) * sign).astype(np.float32)
    g = np.arange(PAIRS0)
    key = np.concatenate([[0, 1], np.stack([3 * g + 2, 3 * g + 3], axis=1).reshape(-1), [T_PAD, T_PAD]])
    tok = np.arange(T_PAD).reshape(TPB, ROWS)
    d["mask0"] = np.where(key[None, None, :] <= tok.T[:, :, None], 0.0, NEG).astype(np.float32)
    d["pkwq"] = a["L0_ffn_Wq"].T
    d["pkkeys"] = a["L0_ffn_keys"].transpose(1, 3, 0, 2).reshape(C, PK_HEADS * C)
    d["tables"] = np.concatenate([a["L0_ffn_w_down_embed"], a["L0_ffn_w_up_embed"]], axis=1)
    wqkv = a["L1_attn_w_qkv"]
    d["a1w"] = np.stack([wqkv[:, 0:C], wqkv[:, C:2 * C], wqkv[:, 2 * C:], a["L1_attn_w_o"]], axis=1)
    d["Wg"] = a["L1_ffn_Wg"]
    d["W1"] = a["L1_ffn_W1"].transpose(1, 0, 2).reshape(C, FCH, C)
    d["W2"] = a["L1_ffn_W2"].reshape(FCH, C, C).transpose(1, 0, 2)
    return {k: np.ascontiguousarray(v) for k, v in d.items()}


def kernel(**inputs):
    import concourse.bacc as bacc
    from concourse.bass_utils import run_bass_kernel_spmd

    arrays = {f"in_{k}": v for k, v in layouts(inputs).items()}
    nc = bacc.Bacc("TRN2", target_bir_lowering=False, num_devices=1)
    t = {k.removeprefix("in_"): nc.dram_tensor(k, v.shape, mybir.dt.from_np(v.dtype), kind="ExternalInput").ap()
         for k, v in arrays.items()}
    t["out"] = nc.dram_tensor("out", (B, T_REAL, C), F32, kind="ExternalOutput").ap()
    audio_tower(nc, t)
    r = run_bass_kernel_spmd(nc, [arrays], core_ids=[0])
    return r.results[0]["out"]
```

```python
from contextlib import ExitStack

import concourse.bass as bass
from concourse import mybir

F32 = mybir.dt.float32
U32 = mybir.dt.uint32
ALU = mybir.AluOpType
ACT = mybir.ActivationFunctionType
AX = mybir.AxisListType

B, T_IN, D_IN = 4, 750, 23
CONTEXT = 5
T_REAL = T_IN - CONTEXT + 1
C = 128
ROWS = 125
TPB = 6
NT = B * TPB
T_PAD = ROWS * TPB
TOK = B * T_PAD
HALF = T_REAL // 2
HALF_PAD = T_PAD // 2
H, DH = 8, 16
EPS = 1e-5
KEYS0 = 498
PAIRS0 = (KEYS0 - 2) // 2
KEYS0_PAD = 500
VW = DH + 1
PK_HEADS, PK_TOP = 8, 8
PK_ROWS = PK_HEADS * PK_TOP
RING = 16
NEG = -1.0e30
SCALE0 = DH ** -0.5
SCALE1 = C ** -0.5
EXPERTS, FF = 8, 512
FCH = EXPERTS * FF // C
GROUP = 500
TILES = H * TPB
PIECES = TILES // TPB
FF_RING = 5
N_LOADS = 11
GELU_A, GELU_B = 0.7978845608028654, 0.044715


def audio_tower(nc, t):
    with ExitStack() as ctx:
        def sb(name, shape, dt=F32):
            return ctx.enter_context(nc.sbuf_tensor(name, shape, dt))

        def sem(name):
            return ctx.enter_context(nc.semaphore(name))

        h_tok = sb("h_tok", [ROWS, NT, C])
        xn_tok = sb("xn_tok", [ROWS, NT, C])
        xT = sb("xT", [C, TOK + ROWS])
        o_cm = sb("o_cm", [C, TOK])
        o_half = sb("o_half", [VW, 2, HALF_PAD])
        sums = sb("sums", [TPB * H, B * ROWS])
        spread = sb("spread", [TPB * H, TPB, C])
        v_b = sb("v_b", [ROWS, H, TPB, VW])
        QKb = sb("QKb", [C, 2, T_PAD])
        QTb, KTb = QKb[:, 0, :], QKb[:, 1, :]
        att = sb("att", [C, 9 * T_PAD])
        arena = sb("arena", [C, 16384])
        qk_slot = [sb(f"qk_slot{s}", [DH, 2, T_PAD]) for s in range(2)]
        q_slot, k_slot = ([slot[:, w, :] for slot in qk_slot] for w in range(2))
        ident = sb("ident", [C, C])
        iota8 = sb("iota8", [C, PK_TOP])
        ones_row = sb("ones_row", [1, ROWS])
        tokw = sb("tokw", [CONTEXT * D_IN, C])
        cols = sb("cols", [C, 64])
        a0w = sb("a0w", [C, 6, C])
        rows1 = sb("rows1", [1, 4, C])
        pkwq = sb("pkwq", [C, PK_HEADS * C])
        pkkeys = sb("pkkeys", [C, PK_HEADS * C])
        a1w = sb("a1w", [C, 4, C])
        wg = sb("wg", [C, EXPERTS])
        stats = sb("stats", [C, NT, 6])
        mv = sb("mv", [C, NT, 2])
        std = sb("std", [C, NT])
        rstd = sb("rstd", [C, NT])
        bn = sb("bn", [C, 8])
        m16 = sb("m16", [ROWS, 2, 16])
        negmax = sb("negmax", [ROWS, 3])
        qhT = sb("qhT", [C, 4, ROWS])
        s8 = sb("s8", [ROWS, 2, H, 8])
        i8 = sb("i8", [ROWS, 2, H, 8], U32)
        i8f = sb("i8f", [ROWS, 2, H, 8])
        pair_s = sb("pair_s", [ROWS, H, 64])
        best = sb("best", [ROWS, H, 8])
        pos = sb("pos", [ROWS, H, 8], U32)
        pos_ij = sb("pos_ij", [ROWS, 2, 64], U32)
        onehot = sb("onehot", [ROWS, 2, 64, 8])
        r_ij = sb("r_ij", [ROWS, 2, 64])
        idx = [sb(f"idx{p}", [C, PK_ROWS], U32) for p in range(2)]
        w_next = sb("w_next", [ROWS, H, 8])
        w_cur = sb("w_cur", [ROWS, PK_ROWS])
        pk8 = sb("pk8", [ROWS, H])
        q_cur = sb("q_cur", [ROWS, C])
        xdot = sb("xdot", [ROWS, PK_ROWS])
        gl = sb("gl", [ROWS, 3, 2 * RING])
        vals = sb("vals", [ROWS, PK_ROWS])
        lg = sb("lg", [ROWS, NT, EXPERTS])
        lg_m = sb("lg_m", [ROWS, NT])
        top_p = sb("top_p", [ROWS, NT, EXPERTS])
        p_i = sb("p_i", [ROWS, 2, NT])

        COL = dict(tok_b=0, gamma=1, beta=2, bq=3, bqs=4, bk=5, bks=6, conv=7, conv_b=10,
                   l1q=11, l1k=12, pkbq=13, b1=21, b2=53)

        def col(name, i=0):
            return cols[:, COL[name] + i:COL[name] + i + 1]

        psum = ctx.enter_context(nc.psum_tensor("psum", [C, 8 * 512], F32))
        bank = [psum[:, 512 * i:512 * i + 512] for i in range(8)]
        BANK_PT, BANK_O, BANK_X, BANK_Y, BANK_SUM = 2, 4, 5, 6, 7
        s0_bank = [bank[k] for k in (0, 1, 7)]
        sum_bank = bank[BANK_SUM][0:ROWS, 0:C]

        def A(at, n, p=C):
            return arena[0:p, at:at + n]


        loaded_tok = sem("loaded_tok")
        loaded_all = sem("loaded_all")
        loaded_ffn = sem("loaded_ffn")
        arrived = sem("arrived")
        go_pe = sem("go_pe")
        go_act = sem("go_act")
        mm_ready = sem("mm_ready")
        mm_ready_v = sem("mm_ready_v")
        act_ready = sem("act_ready")
        act_ready_pe = sem("act_ready_pe")
        dve_ready = sem("dve_ready")
        dve_to_act = sem("dve_to_act")
        dve_self = sem("dve_self")
        act_self = sem("act_self")
        top_self = sem("top_self")
        pk_self = sem("pk_self")
        q_used = sem("q_used")
        k_used = sem("k_used")
        qk_here = sem("qk_here")
        slot_loaded = [sem(f"slot_loaded{s}") for s in range(2)]
        slot_free = [sem(f"slot_free{s}") for s in range(2)]
        s_ready = sem("s_ready")
        s_free = sem("s_free")
        s_here = sem("s_here")
        s_masked = sem("s_masked")
        s_max = sem("s_max")
        e_ready = sem("e_ready")
        p_ready = sem("p_ready")
        t_ready = sem("t_ready")
        pt_ready = sem("pt_ready")
        o_ready = sem("o_ready")
        o_free = sem("o_free")
        o_here = sem("o_here")
        o_moved = [sem(f"o_moved{f}") for f in range(2)]
        qh_ready = sem("qh_ready")
        qh_here = sem("qh_here")
        scores_ready = sem("scores_ready")
        scores_free = sem("scores_free")
        exp_in = sem("exp_in")
        exp_out = sem("exp_out")
        tanh_in = sem("tanh_in")
        tanh_out = sem("tanh_out")
        idx_ready = sem("idx_ready")
        gathered = [sem(f"gathered{c}") for c in range(4)]
        ring_free = [sem(f"ring_free{c}") for c in range(4)]
        vals_ready = sem("vals_ready")
        up_ready = sem("up_ready")
        usum_ready = sem("usum_ready")
        usum_free = sem("usum_free")
        memory_done = sem("memory_done")
        z_ready = sem("z_ready")
        zg_ready = sem("zg_ready")
        g_ready = sem("g_ready")
        gs_ready = sem("gs_ready")
        chunk_done = sem("chunk_done")
        h_done = sem("h_done")
        stored = sem("stored")

        patches = A(0, B * T_REAL, CONTEXT * D_IN).rearrange("p (b n) -> p b n", b=B)
        yT = A(3000, TOK)
        cosT, sinT = A(6000, T_PAD), A(6750, T_PAD)
        mask0 = A(7500, TPB * KEYS0_PAD, ROWS).rearrange("p (i n) -> p i n", i=TPB)
        rot_q, rot_k = ([A(at, T_PAD), A(at + T_PAD, T_PAD)] for at in (10500, 12500))
        xc = A(12000, KEYS0_PAD)
        G = arena[:, :].rearrange("p (k r d) -> p k r d", k=4, r=RING)
        w1 = A(0, FCH * C).rearrange("p (m c) -> p m c", m=FCH)
        w2 = A(4096, FCH * C).rearrange("p (m c) -> p m c", m=FCH)
        gate = A(8192, 2 * TOK).rearrange("p (i n) -> p i n", i=2)

        def T(k, p=ROWS, n=T_PAD):
            return att[0:p, T_PAD * k:T_PAD * k + n]

        sm0 = [T(k) for k in range(3)]
        s1 = [T(0), T(8)]
        w_b = [T(1), T(2)]
        pr = [T(3 + k) for k in range(3)]
        pt = [T(6), T(7)]
        xn_b = att[0:ROWS, 0:TPB * C].rearrange("p (i c) -> p i c", i=TPB)
        xTb, conv_t, conv_x = T(2, C), T(3, C), T(4, C)
        zg = [att[:, 2 * GROUP * k:2 * GROUP * (k + 1)].rearrange("p (i n) -> p i n", i=2) for k in range(FF_RING)]
        at = 2 * GROUP * FF_RING
        g_sum = [att[:, at:at + GROUP]] + [A(14192 + GROUP * k, GROUP) for k in range(FF_RING - 1)]
        yT_ffn = att[:, at + GROUP:at + 2 * GROUP]
        z_bank = [bank[k] for k in (0, 1, 2, 3, 6)]

        visible = [sum(1 for s in range(T_REAL) if s <= ROWS * i + ROWS - 1 and not (s >= 4 and s % 3 == 1))
                   for i in range(TPB)]
        chunks0 = [-(-v // ROWS) for v in visible]

        def n_chunks(layer, n):
            return chunks0[n % TPB] if layer == 0 else TPB

        def mix_steps(k):
            return [(i, k - PIECES * i - 4) for i in range(TPB) if 0 <= k - PIECES * i - 4 <= 9]

        STEPS = TILES + 6

        def rank_step(k):
            return divmod(k, PIECES) if k < TILES else (None, None)

        block = ctx.enter_context(nc.Block())

        @block.sync
        def _(sp):
            for k in range(CONTEXT):
                sp.dma_start(patches[D_IN * k:D_IN * (k + 1), :, :],
                             t["x"][:, :, k:k + T_REAL]).then_inc(loaded_tok, 16)
            sp.dma_start(tokw[:, :], t["tok_W"]).then_inc(loaded_tok, 16)
            sp.dma_start(cols[:, :], t["cols"]).then_inc(loaded_tok, 16)
            sp.dma_start(ident[:, :], t["ident"]).then_inc(loaded_tok, 16)
            loads = ((a0w[:, :, :], t["a0w"]), (rows1[:, :, :], t["rows1"]),
                     (cosT, t["cosT"]), (sinT, t["sinT"]), (mask0, t["mask0"]), (iota8[:, :], t["iota8"]),
                     (pkwq[:, :], t["pkwq"]), (pkkeys[:, :], t["pkkeys"]),
                     (a1w[:, :, :], t["a1w"]), (spread[:, :, :], t["spread"]), (wg[:, :], t["Wg"]))
            assert len(loads) == N_LOADS
            for dst, src in loads:
                sp.dma_start(dst, src).then_inc(loaded_all, 16)

            def heads(b):
                def load(h):
                    s = h % 2
                    sp.wait_ge(slot_free[s], 1)
                    sp.sem_inc(slot_free[s], -1)
                    sp.dma_start(qk_slot[s][:, :, :],
                                 QKb[DH * h:DH * (h + 1), :, :]).then_inc(slot_loaded[s], 16)

                sp.wait_ge(qk_here, 1)
                sp.sem_inc(qk_here, -1)
                load(0)
                load(1)
                for h in range(H):
                    for f in range(2):
                        sp.wait_ge(o_here, 1)
                        sp.sem_inc(o_here, -1)
                        sp.dma_start(o_cm[DH * h:DH * (h + 1), bass.ds(b * T_PAD + HALF_PAD * f, HALF_PAD)],
                                     o_half[0:DH, f, :]).then_inc(o_moved[f], 16)
                        row = 3 * H * f + h
                        sp.dma_start(sums[row:row + 2 * H + 1:H, bass.ds(b * ROWS, ROWS)],
                                     o_half[DH:VW, f, :]).then_inc(o_moved[f], 16)
                        if f == 0 and h + 2 < H:
                            load(h + 2)

            with sp.Fori(0, B) as b:
                heads(b)
            with sp.Fori(0, B - 1) as b:
                heads(b)
            sp.wait_ge(memory_done, 1)
            sp.sem_inc(memory_done, -1)
            sp.dma_start(w1, t["W1"]).then_inc(loaded_ffn, 16)
            sp.dma_start(w2, t["W2"]).then_inc(loaded_ffn, 16)
            heads(B - 1)
            sp.wait_ge(h_done, 1)
            sp.sem_inc(h_done, -1)
            for b in range(B):
                full = ROWS * (TPB - 1)
                sp.dma_start(t["out"][b, 0:full, :].rearrange("(i p) c -> p i c", p=ROWS),
                             h_tok[:, TPB * b:TPB * b + TPB - 1, :]).then_inc(stored, 16)
                sp.dma_start(t["out"][b, full:T_REAL, :],
                             h_tok[0:T_REAL - full, TPB * b + TPB - 1, :]).then_inc(stored, 16)
            sp.wait_ge(stored, 16 * 2 * B)

        @block.tensor
        def _(pe):
            def meet():
                pe.drain().then_inc(arrived, 1)
                pe.wait_ge(go_pe, 1)
                pe.sem_inc(go_pe, -1)

            def norm_transpose():
                for j in range(NT // 4):
                    pe.wait_ge(dve_ready, 1)
                    pe.sem_inc(dve_ready, -1)
                    for k in range(4):
                        ins = pe.transpose(bank[j][:, ROWS * k:ROWS * (k + 1)], xn_tok[:, 4 * j + k, :],
                                           ident[0:ROWS, 0:ROWS])
                    ins.then_inc(mm_ready, 1)

            def scores(layer, n):
                h, i = divmod(n, TPB)
                s = h % 2
                if i == 0:
                    pe.wait_ge(slot_loaded[s], 16)
                    pe.sem_inc(slot_loaded[s], -16)
                lhsT = q_slot[s][:, ROWS * i:ROWS * (i + 1)]
                if layer == 0:
                    w = ROWS * chunks0[i]
                    pe.matmul(s0_bank[n % 3][0:ROWS, 0:w], lhsT, k_slot[s][:, 0:w],
                              start=True, stop=True).then_inc(s_ready, 1)
                else:
                    pe.wait_ge(s_free, 1)
                    pe.sem_inc(s_free, -1)
                    pe.matmul(bank[0][0:ROWS, :], lhsT, k_slot[s][:, 0:512], start=True, stop=True)
                    pe.matmul(bank[1][0:ROWS, 0:T_REAL - 512], lhsT, k_slot[s][:, 512:T_REAL],
                              start=True, stop=True).then_inc(s_ready, 1)

            def transposes(layer, n):
                if n:
                    pe.wait_ge(pt_ready, 1)
                    pe.sem_inc(pt_ready, -1)
                pe.wait_ge(p_ready, 1)
                pe.sem_inc(p_ready, -1)
                for c in range(n_chunks(layer, n)):
                    if layer == 0:
                        dst = bank[BANK_PT + n % 2][0:ROWS, ROWS * c:ROWS * (c + 1)]
                    else:
                        dst = bank[BANK_PT + c // 3][0:ROWS, ROWS * (c % 3):ROWS * (c % 3 + 1)]
                    ins = pe.transpose(dst, pr[n % 3][:, ROWS * c:ROWS * (c + 1)], ident[0:ROWS, 0:ROWS])
                ins.then_inc(t_ready, 1)

            def values(layer, n):
                h, i = divmod(n, TPB)
                if n == TILES - 1:
                    pe.wait_ge(pt_ready, 1)
                    pe.sem_inc(pt_ready, -1)
                if i % 3 == 0:
                    pe.wait_ge(o_free, 1)
                    pe.sem_inc(o_free, -1)
                last = n_chunks(layer, n) - 1
                for c in range(last + 1):
                    ins = pe.matmul(bank[BANK_O][0:VW, ROWS * (i % 3):ROWS * (i % 3 + 1)], v_b[:, h, c, :],
                                    pt[n % 2][:, ROWS * c:ROWS * (c + 1)],
                                    start=(c == 0), stop=(c == last))
                if i % 3 == 2:
                    ins.then_inc(o_ready, 1)

            def pk_queries(g, n):
                pe.wait_ge(scores_free, 1)
                pe.sem_inc(scores_free, -1)
                for hh in range(4):
                    ins = pe.matmul(bank[BANK_X][:, ROWS * hh:ROWS * (hh + 1)],
                                    pkwq[:, C * (4 * g + hh):C * (4 * g + hh + 1)], xT[:, bass.ds(n * ROWS, ROWS)],
                                    start=True, stop=True)
                ins.then_inc(qh_ready, 1)

            def pk_scores(g):
                pe.wait_ge(qh_here, 1)
                pe.sem_inc(qh_here, -1)
                for c, bk in ((0, BANK_Y), (1, BANK_X)):
                    for hh in range(4):
                        h = 4 * g + hh
                        ins = pe.matmul(bank[bk][0:ROWS, C * hh:C * (hh + 1)], qhT[64 * c:64 * (c + 1), hh, :],
                                        pkkeys[64 * c:64 * (c + 1), C * h:C * (h + 1)], start=True, stop=True)
                ins.then_inc(scores_ready, 1)

            def pk_sum(c):
                pe.wait_ge(usum_free, 1)
                pe.sem_inc(usum_free, -1)
                pe.wait_ge(up_ready, 1)
                pe.sem_inc(up_ready, -1)
                for r in range(RING):
                    ins = pe.matmul(sum_bank, ident[0:ROWS, 0:ROWS], G[0:ROWS, c, r, C:2 * C],
                                    start=(r == 0), stop=(r == RING - 1))
                ins.then_inc(usum_ready, 1)

            def pk_rank_piece(r, n):
                if r in (0, 3):
                    pk_queries(r // 3, n)
                if r in (1, 4):
                    pk_scores(r // 3)

            def steps(layer, b=None):
                if layer is not None:
                    scores(layer, 0)
                if layer == 0:
                    scores(layer, 1)
                for k in range(STEPS):
                    if layer == 1 and k + 1 < TILES:
                        scores(1, k + 1)
                    if b is not None:
                        i, r = rank_step(k)
                        if i is not None:
                            pk_rank_piece(r, b * TPB + (i + 1))
                        for _, u in mix_steps(k):
                            if u in (3, 4, 7, 8):
                                pk_sum({3: 0, 4: 1, 7: 2, 8: 3}[u])
                    if layer is not None and 1 <= k <= TILES:
                        transposes(layer, k - 1)
                    if layer == 0 and k + 2 < TILES:
                        scores(0, k + 2)
                    if layer is not None and 2 <= k <= TILES + 1:
                        values(layer, k - 2)

            def attention_out(w_o, b_row):
                pe.wait_ge(dve_ready, 1)
                pe.sem_inc(dve_ready, -1)
                for j in range(NT // 4):
                    for k in range(4):
                        b, i = divmod(4 * j + k, TPB)
                        ins = pe.matmul(bank[j][:, ROWS * k:ROWS * (k + 1)], spread[:, i, :],
                                        sums[:, ROWS * b:ROWS * (b + 1)], start=True, stop=True)
                    ins.then_inc(mm_ready_v, 1)
                for j in range(NT // 4):
                    pe.wait_ge(dve_ready, 1)
                    pe.sem_inc(dve_ready, -1)
                    for k in range(4):
                        n = 4 * j + k
                        dst = bank[j][0:ROWS, C * k:C * (k + 1)]
                        pe.matmul(dst, o_cm[:, ROWS * n:ROWS * (n + 1)], w_o, start=True, stop=False)
                        ins = pe.matmul(dst, ones_row[:, :], b_row, start=False, stop=True)
                    ins.then_inc(mm_ready_v, 1)
                meet()

            pe.wait_ge(loaded_tok, 16 * 8)
            for j in range(2 * B):
                b, f = divmod(j, 2)
                pe.matmul(bank[j][:, 0:HALF], tokw[:, :], patches[:, b, HALF * f:HALF * (f + 1)],
                          start=True, stop=True).then_inc(mm_ready, 1)
            pe.wait_ge(dve_ready, 1)
            pe.sem_inc(dve_ready, -1)
            for j in range(NT // 4):
                for k in range(4):
                    n = 4 * j + k
                    ins = pe.transpose(bank[j][0:ROWS, C * k:C * (k + 1)], yT[:, ROWS * n:ROWS * (n + 1)],
                                       ident[:, :])
                ins.then_inc(mm_ready_v, 1)
            meet()
            norm_transpose()
            meet()
            pe.wait_ge(loaded_all, 16 * N_LOADS)
            with pe.Fori(0, B) as b:
                for w in range(2):
                    for f in range(2):
                        ins = pe.matmul(bank[2 * w + f][:, 0:375], a0w[:, w, :],
                                        xT[:, bass.ds(b * T_PAD + 375 * f, 375)], start=True, stop=True)
                ins.then_inc(mm_ready_v, 1)
                for w in range(2, 4):
                    for f in range(2):
                        ins = pe.matmul(bank[2 * w + f][:, 0:375], a0w[:, w, :],
                                        xT[:, bass.ds(b * T_PAD + 375 * f, 375)], start=True, stop=True)
                ins.then_inc(mm_ready_v, 1)
                pe.wait_ge(q_used, 1)
                pe.sem_inc(q_used, -1)
                for c in range(4):
                    dst = bank[0][0:ROWS, C * c:C * (c + 1)]
                    pe.matmul(dst, xc[:, ROWS * c:ROWS * (c + 1)], a0w[:, 4, :], start=True, stop=False)
                    ins = pe.matmul(dst, ones_row[:, :], rows1[:, 0, :], start=False, stop=True)
                ins.then_inc(mm_ready, 1)
                meet()
                steps(0)
                meet()
            meet()
            attention_out(a0w[:, 5, :], rows1[:, 1, :])
            norm_transpose()
            meet()

            def project1():
                pe.wait_ge(dve_ready, 1)
                pe.sem_inc(dve_ready, -1)
                for i in range(TPB):
                    ins = pe.transpose(bank[i // 4][:, ROWS * (i % 4):ROWS * (i % 4 + 1)], xn_b[:, i, :],
                                       ident[0:ROWS, 0:ROWS])
                ins.then_inc(mm_ready, 1)
                pe.wait_ge(dve_ready, 1)
                pe.sem_inc(dve_ready, -1)
                for w in range(2):
                    for f in range(2):
                        ins = pe.matmul(bank[2 + 2 * w + f][:, 0:375], a1w[:, w, :],
                                        conv_x[:, 375 * f:375 * (f + 1)], start=True, stop=True)
                ins.then_inc(mm_ready, 1)
                for c in range(TPB):
                    dst = bank[6 + c // 3][0:ROWS, C * (c % 3):C * (c % 3 + 1)]
                    pe.matmul(dst, conv_x[:, ROWS * c:ROWS * (c + 1)], a1w[:, 2, :], start=True, stop=False)
                    ins = pe.matmul(dst, ones_row[:, :], rows1[:, 2, :], start=False, stop=True)
                ins.then_inc(mm_ready_v, 1)
                meet()

            for r in range(PIECES):
                pk_rank_piece(r, 0)
            steps(None, 0)
            meet()
            project1()
            with pe.Fori(1, B) as b:
                steps(1, b)
                meet()
                project1()
            steps(1)
            meet()
            attention_out(a1w[:, 3, :], rows1[:, 3, :])

            norm_transpose()
            for j in range(NT // 4):
                pe.wait_ge(act_ready_pe, 1)
                pe.sem_inc(act_ready_pe, -1)
                for k in range(4):
                    n = 4 * j + k
                    ins = pe.matmul(bank[7][0:ROWS, EXPERTS * n:EXPERTS * (n + 1)],
                                    xT[:, ROWS * n:ROWS * (n + 1)], wg[:, :], start=True, stop=True)
            ins.then_inc(mm_ready_v, 1)
            pe.wait_ge(dve_ready, 1)
            pe.sem_inc(dve_ready, -1)
            for j in range(NT // 4):
                for i in range(2):
                    if j >= 2:
                        pe.wait_ge(act_ready_pe, 1)
                        pe.sem_inc(act_ready_pe, -1)
                    for k in range(4):
                        ins = pe.matmul(bank[2 * (j % 2) + i][:, ROWS * k:ROWS * (k + 1)],
                                        p_i[:, i, 4 * j + k:4 * j + k + 1].to_broadcast([ROWS, C]),
                                        ident[0:ROWS, 0:ROWS], start=True, stop=True)
                    ins.then_inc(mm_ready, 1)
            for _ in range(4):
                pe.wait_ge(act_ready_pe, 1)
                pe.sem_inc(act_ready_pe, -1)
            meet()

            pe.wait_ge(loaded_ffn, 32)
            with pe.Fori(0, TOK // GROUP) as g:
                def hidden(m):
                    pe.matmul(z_bank[m % FF_RING][:, 0:GROUP], w1[:, m, :], xT[:, bass.ds(g * GROUP, GROUP)],
                              start=True, stop=True).then_inc(z_ready, 1)

                for m in range(FF_RING - 1):
                    hidden(m)
                for m in range(FCH):
                    pe.wait_ge(gs_ready, 1)
                    pe.sem_inc(gs_ready, -1)
                    pe.matmul(bank[4][:, 0:GROUP], w2[:, m, :], g_sum[m % FF_RING],
                              start=(m == 0), stop=(m == FCH - 1)).then_inc(chunk_done, 1)
                    if m + FF_RING - 1 < FCH:
                        hidden(m + FF_RING - 1)
                pe.wait_ge(dve_ready, 1)
                pe.sem_inc(dve_ready, -1)
                for k in range(4):
                    ins = pe.transpose(bank[5][0:ROWS, C * k:C * (k + 1)], yT_ffn[:, ROWS * k:ROWS * (k + 1)],
                                       ident[:, :])
                ins.then_inc(mm_ready_v, 1)
            meet()

        @block.scalar
        def _(act):
            def meet():
                act.drain().then_inc(arrived, 1)
                act.wait_ge(go_act, 1)
                act.sem_inc(go_act, -1)

            def norm_part(to_pe=False):
                act.wait_ge(dve_to_act, 1)
                act.sem_inc(dve_to_act, -1)
                act.activation(std[0:ROWS, :], std[0:ROWS, :], ACT.Sqrt).then_inc(act_ready, 1)
                for j in range(NT // 4):
                    act.wait_ge(mm_ready, 1)
                    act.sem_inc(mm_ready, -1)
                    ins = act.copy(xT[:, GROUP * j:GROUP * (j + 1)], bank[j][:, 0:GROUP])
                    if to_pe:
                        ins.then_inc(act_ready_pe, 1)

            def exp0(n):
                w = ROWS * chunks0[n % TPB]
                act.wait_ge(s_masked, 1)
                act.sem_inc(s_masked, -1)
                act.activation(pr[n % 3][:, 0:w], sm0[n % 3][:, 0:w], ACT.Exp,
                               bias=negmax[:, n % 3:n % 3 + 1], scale=-1.0).then_inc(p_ready, 1)

            def exp_all(n):
                act.wait_ge(s_max, 1)
                act.sem_inc(s_max, -1)
                act.activation(pr[n % 3][:, 0:T_REAL], s1[n % 2][:, 0:T_REAL], ACT.Exp,
                               bias=negmax[:, n % 3:n % 3 + 1], scale=SCALE1).then_inc(e_ready, 1)

            def copy_scores(n):
                act.wait_ge(s_ready, 1)
                act.sem_inc(s_ready, -1)
                act.copy(s1[n % 2][:, 0:T_REAL], psum[0:ROWS, 0:T_REAL]).then_inc(s_here, 1)

            def move(layer, n):
                act.wait_ge(t_ready, 1)
                act.sem_inc(t_ready, -1)
                if layer == 0:
                    w = ROWS * chunks0[n % TPB]
                    act.copy(pt[n % 2][:, 0:w], bank[BANK_PT + n % 2][0:ROWS, 0:w]).then_inc(pt_ready, 1)
                else:
                    both = psum[0:ROWS, 512 * BANK_PT:512 * (BANK_PT + 2)].rearrange("p (a n) -> p a n", a=2)
                    act.copy(pt[n % 2].rearrange("p (a n) -> p a n", a=2),
                             both[:, :, 0:375]).then_inc(pt_ready, 1)

            def half_out(h, f):
                act.wait_ge(o_ready, 1)
                act.sem_inc(o_ready, -1)
                act.wait_ge(o_moved[f], 32)
                act.sem_inc(o_moved[f], -32)
                act.copy(o_half[:, f, :], bank[BANK_O][0:VW, 0:HALF_PAD]).then_inc(act_self, 1)
                act.wait_ge(act_self, 1)
                act.sem_inc(act_self, -1)
                act.sem_inc(o_free, 1)
                act.sem_inc(o_here, 1)

            def pk_queries(g):
                act.wait_ge(qh_ready, 1)
                act.sem_inc(qh_ready, -1)
                for hh in range(4):
                    ins = act.activation(qhT[:, hh, :], bank[BANK_X][:, ROWS * hh:ROWS * (hh + 1)],
                                         ACT.Identity, bias=col("pkbq", 4 * g + hh))
                ins.then_inc(qh_here, 1)

            def pk_exp():
                act.wait_ge(exp_in, 1)
                act.sem_inc(exp_in, -1)
                act.activation(w_next[:, :, :], w_next[:, :, :], ACT.Exp).then_inc(exp_out, 1)

            def pk_tanh():
                act.wait_ge(tanh_in, 1)
                act.sem_inc(tanh_in, -1)
                act.activation(gl[:, 2, :], gl[:, 0, :], ACT.Tanh, scale=GELU_A).then_inc(tanh_out, 1)

            def pk_up(c):
                if c % 2 == 0:
                    act.wait_ge(vals_ready, 1)
                    act.sem_inc(vals_ready, -1)
                for r in range(RING):
                    up = G[0:ROWS, c, r, C:2 * C]
                    k = RING * c + r
                    ins = act.activation(up, up, ACT.Copy, scale=vals[:, k:k + 1])
                ins.then_inc(up_ready, 1)

            def pk_rank_piece(r):
                if r in (0, 3):
                    pk_queries(r // 3)
                if r == 6:
                    pk_exp()

            def steps(layer, memory=False):
                if layer == 1:
                    copy_scores(0)
                for k in range(STEPS):
                    if layer is not None and 5 <= k < TILES + 3 and k % 3 == 2:
                        half_out(*divmod(k // 3 - 1, 2))
                    if layer == 0:
                        if k < TILES:
                            exp0(k)
                        if 1 <= k <= TILES:
                            move(0, k - 1)
                    if layer == 1:
                        if 2 <= k <= TILES + 1:
                            move(1, k - 2)
                        if k < TILES:
                            exp_all(k)
                        if k + 1 < TILES:
                            copy_scores(k + 1)
                    if memory:
                        for _, u in mix_steps(k):
                            if u in (1, 5):
                                pk_tanh()
                        i, r = rank_step(k)
                        if i is not None:
                            pk_rank_piece(r)
                        for _, u in mix_steps(k):
                            if u in (2, 3, 6, 7):
                                pk_up({2: 0, 3: 1, 6: 2, 7: 3}[u])

            act.wait_ge(loaded_tok, 16 * 8)
            for j in range(2 * B):
                b, f = divmod(j, 2)
                at = T_PAD * b + HALF * f
                act.wait_ge(mm_ready, 1)
                act.sem_inc(mm_ready, -1)
                act.activation(yT[:, at:at + HALF], bank[j][:, 0:HALF], ACT.Relu,
                               bias=col("tok_b")).then_inc(act_ready, 1)
            act.wait_ge(dve_to_act, 1)
            act.sem_inc(dve_to_act, -1)
            act.activation(bn[:, 2:3], bn[:, 2:3], ACT.Sqrt).then_inc(act_ready, 1)
            meet()
            norm_part()
            meet()
            act.sem_inc(o_free, 1)
            for f in range(2):
                act.sem_inc(o_moved[f], 32)
            with act.Fori(0, B):
                act.wait_ge(mm_ready, 1)
                act.sem_inc(mm_ready, -1)
                act.copy(v_b[:, :, 0:4, 0:DH].rearrange("p h c d -> p c h d"),
                         bank[0][0:ROWS, :].rearrange("p (c h d) -> p c h d", c=4, h=H))
                meet()
                steps(0)
                meet()
            for f in range(2):
                act.wait_ge(o_moved[f], 32)
            meet()
            meet()
            norm_part()
            meet()

            def project1():
                act.wait_ge(dve_to_act, 1)
                act.sem_inc(dve_to_act, -1)
                act.activation(std[0:ROWS, 0:TPB], std[0:ROWS, 0:TPB], ACT.Sqrt).then_inc(act_ready, 1)
                act.wait_ge(mm_ready, 1)
                act.sem_inc(mm_ready, -1)
                act.copy(xTb[:, 0:GROUP], bank[0][:, 0:GROUP])
                act.copy(xTb[:, GROUP:T_PAD], bank[1][:, 0:T_PAD - GROUP]).then_inc(act_ready, 1)
                act.wait_ge(mm_ready, 1)
                act.sem_inc(mm_ready, -1)
                for w, (dst, bias) in enumerate(((QTb, col("l1q")), (KTb, col("l1k")))):
                    for f in range(2):
                        ins = act.activation(dst[:, 375 * f:375 * (f + 1)], bank[2 + 2 * w + f][:, 0:375],
                                             ACT.Identity, bias=bias)
                ins.then_inc(qk_here, 1)
                meet()

            for r in range(PIECES):
                pk_rank_piece(r)
            steps(None, True)
            meet()
            project1()
            with act.Fori(1, B):
                steps(1, True)
                meet()
                project1()
            steps(1)
            for f in range(2):
                act.wait_ge(o_moved[f], 32)
            meet()
            meet()
            norm_part(True)
            act.wait_ge(dve_to_act, 1)
            act.sem_inc(dve_to_act, -1)
            act.activation(lg[:, :, :], lg[:, :, :], ACT.Exp).then_inc(act_ready, 1)
            for j in range(NT // 4):
                for i in range(2):
                    act.wait_ge(mm_ready, 1)
                    act.sem_inc(mm_ready, -1)
                    act.copy(gate[:, i, GROUP * j:GROUP * (j + 1)],
                             bank[2 * (j % 2) + i][:, 0:GROUP]).then_inc(act_ready_pe, 1)
            meet()
            with act.Fori(0, TOK // GROUP):
                for m in range(FCH):
                    act.wait_ge(zg_ready, 1)
                    act.sem_inc(zg_ready, -1)
                    act.activation(zg[m % FF_RING], zg[m % FF_RING], ACT.Gelu,
                                   bias=col("b1", m)).then_inc(g_ready, 1)
            meet()

        @block.vector
        def _(dve):
            def settle(ins):
                ins.then_inc(dve_self, 1)
                dve.wait_ge(dve_self, 1)
                dve.sem_inc(dve_self, -1)

            def meet():
                settle(dve.drain())
                dve.wait_ge(arrived, 2)
                dve.sem_inc(arrived, -2)
                dve.sem_inc(go_pe, 1)
                dve.sem_inc(go_act, 1)

            def norm_part():
                for n in range(NT):
                    ins = dve.bn_stats(stats[0:ROWS, n, :], h_tok[:, n, :])
                settle(ins)
                for n in range(NT):
                    ins = dve.bn_aggr(mv[0:ROWS, n, :], stats[0:ROWS, n, :])
                settle(ins)
                dve.tensor_scalar(std[0:ROWS, :], mv[0:ROWS, :, 1], EPS, None, ALU.add).then_inc(dve_to_act, 1)
                dve.wait_ge(act_ready, 1)
                dve.sem_inc(act_ready, -1)
                settle(dve.reciprocal(rstd[0:ROWS, :], std[0:ROWS, :]))
                for n in range(NT):
                    ins = dve.tensor_scalar(xn_tok[:, n, :], h_tok[:, n, :], mv[0:ROWS, n, 0:1],
                                            rstd[0:ROWS, n:n + 1], ALU.subtract, ALU.mult)
                    if n % 4 == 3:
                        ins.then_inc(dve_ready, 1)

            def mask_and_max(n):
                i = n % TPB
                w = ROWS * chunks0[i]
                dve.wait_ge(s_ready, 1)
                dve.sem_inc(s_ready, -1)
                if i == TPB - 1:
                    dve.sem_inc(slot_free[n // TPB % 2], 1)
                dve.tensor_tensor_reduce(sm0[n % 3][:, 0:w], s0_bank[n % 3][0:ROWS, 0:w], mask0[:, i, 0:w],
                                         -SCALE0, -NEG, ALU.add, ALU.min,
                                         negmax[:, n % 3:n % 3 + 1]).then_inc(s_masked, 1)

            def top16(n):
                s_n, w_n, p_n = (a[:, 0:T_REAL] for a in (s1[n % 2], w_b[n % 2], pr[n % 3]))
                top = m16[:, n % 2, :]
                dve.wait_ge(s_here, 1)
                dve.sem_inc(s_here, -1)
                dve.sem_inc(s_free, 1)
                if n % TPB == TPB - 1:
                    dve.sem_inc(slot_free[n // TPB % 2], 1)
                dve.max(top[:, 0:8], s_n).then_inc(top_self, 1)
                yield
                dve.wait_ge(top_self, 1)
                dve.sem_inc(top_self, -1)
                dve.tensor_scalar(negmax[:, n % 3:n % 3 + 1], top[:, 0:1], -SCALE1, None,
                                  ALU.mult).then_inc(s_max, 1)
                dve.match_replace(w_n, top[:, 0:8], s_n, NEG).then_inc(top_self, 1)
                yield
                dve.wait_ge(top_self, 1)
                dve.sem_inc(top_self, -1)
                dve.max(top[:, 8:16], w_n).then_inc(top_self, 1)
                yield
                dve.wait_ge(top_self, 1)
                dve.sem_inc(top_self, -1)
                dve.match_replace(w_n, top[:, 8:16], w_n, NEG).then_inc(top_self, 1)
                yield
                dve.wait_ge(top_self, 1)
                dve.sem_inc(top_self, -1)
                dve.wait_ge(e_ready, 1)
                dve.sem_inc(e_ready, -1)
                dve.scalar_tensor_tensor(p_n, w_n, NEG, p_n, ALU.is_equal, ALU.mult).then_inc(p_ready, 1)

            def pk_rank_half(g):
                dve.wait_ge(scores_ready, 1)
                dve.sem_inc(scores_ready, -1)
                at = [(c, 4 * g + hh, bank[bk][0:ROWS, C * hh:C * (hh + 1)])
                      for c, bk in ((0, BANK_Y), (1, BANK_X)) for hh in range(4)]
                for c, h, s in at:
                    ins = dve.max(s8[:, c, h, :], s)
                ins.then_inc(pk_self, 1)
                yield
                dve.wait_ge(pk_self, 1)
                dve.sem_inc(pk_self, -1)
                for c, h, s in at:
                    ins = dve.max_index(i8[:, c, h, :], s8[:, c, h, :], s)
                ins.then_inc(scores_free, 1)

            def pk_pairs():
                dve.tensor_tensor(
             pair_s[:, :, :].rearrange("p h (i j) -> p h i j", i=8),
             s8[:, 0, :, :].unsqueeze(3).to_broadcast([ROWS, H, 8, 8]),
             s8[:, 1, :, :].unsqueeze(2).to_broadcast([ROWS, H, 8, 8]), ALU.add).then_inc(pk_self, 1)
                yield
                dve.wait_ge(pk_self, 1)
                dve.sem_inc(pk_self, -1)
                dve.tensor_copy(i8f[:, :, :, :], i8[:, :, :, :])
                for h in range(PK_HEADS):
                    ins = dve.max(best[:, h, :], pair_s[:, h, :])
                ins.then_inc(pk_self, 1)
                yield
                dve.wait_ge(pk_self, 1)
                dve.sem_inc(pk_self, -1)
                dve.tensor_tensor(w_next[:, :, :], best[:, :, :], best[:, :, 0:1].to_broadcast([ROWS, H, 8]),
                                  ALU.subtract).then_inc(exp_in, 1)
                yield
                for h in range(PK_HEADS):
                    ins = dve.max_index(pos[:, h, :], best[:, h, :], pair_s[:, h, :])
                ins.then_inc(pk_self, 1)
                yield
                dve.wait_ge(pk_self, 1)
                dve.sem_inc(pk_self, -1)

            def pk_rows(parity):
                flat = pos[:, :, :].rearrange("p h k -> p (h k)")
                dve.tensor_scalar(pos_ij[:, 0, :], flat, 3, None, ALU.logical_shift_right)
                dve.tensor_scalar(pos_ij[:, 1, :], flat, 7, None, ALU.bitwise_and).then_inc(pk_self, 1)
                yield
                dve.wait_ge(pk_self, 1)
                dve.sem_inc(pk_self, -1)
                for c in range(2):
                    ins = dve.tensor_tensor(onehot[:, c, :, :],
                                            iota8[0:ROWS, :].unsqueeze(1).to_broadcast([ROWS, 64, 8]),
                                            pos_ij[:, c, :].unsqueeze(2).to_broadcast([ROWS, 64, 8]), ALU.is_equal)
                ins.then_inc(pk_self, 1)
                yield
                dve.wait_ge(pk_self, 1)
                dve.sem_inc(pk_self, -1)
                for c in range(2):
                    oh = onehot[:, c, :, :].rearrange("p (h k) i -> p h k i", h=H)
                    ins = dve.tensor_tensor(oh, oh, i8f[:, c, :, :].unsqueeze(2).to_broadcast([ROWS, H, 8, 8]),
                                            ALU.mult)
                ins.then_inc(pk_self, 1)
                yield
                dve.wait_ge(pk_self, 1)
                dve.sem_inc(pk_self, -1)
                dve.tensor_reduce(r_ij[:, :, :], onehot[:, :, :, :], AX.X, ALU.add).then_inc(pk_self, 1)
                yield
                dve.wait_ge(pk_self, 1)
                dve.sem_inc(pk_self, -1)
                dve.scalar_tensor_tensor(idx[parity][0:ROWS, :], r_ij[:, 0, :], float(C), r_ij[:, 1, :],
                                         ALU.mult, ALU.add).then_inc(idx_ready, 1)

            def pk_softmax():
                dve.wait_ge(exp_out, 1)
                dve.sem_inc(exp_out, -1)
                dve.tensor_reduce(pk8[:, :], w_next[:, :, :], AX.X, ALU.add).then_inc(pk_self, 1)
                yield
                dve.wait_ge(pk_self, 1)
                dve.sem_inc(pk_self, -1)
                dve.reciprocal(pk8[:, :], pk8[:, :]).then_inc(pk_self, 1)
                yield
                dve.wait_ge(pk_self, 1)
                dve.sem_inc(pk_self, -1)
                dve.tensor_tensor(w_next[:, :, :], w_next[:, :, :],
                                  pk8[:, :].unsqueeze(2).to_broadcast([ROWS, H, 8]), ALU.mult).then_inc(pk_self, 1)
                yield
                dve.wait_ge(pk_self, 1)
                dve.sem_inc(pk_self, -1)

            def pk_rank_piece(r, parity):
                if r in (2, 5):
                    yield from pk_rank_half(r // 3)
                if r == 6:
                    yield from pk_pairs()
                if r == 7:
                    yield from pk_rows(parity)
                    yield from pk_softmax()

            def pk_keep(n):
                dve.tensor_copy(w_cur[:, :], w_next[:, :, :].rearrange("p h k -> p (h k)"))
                dve.tensor_copy(q_cur[:, :], xn_tok[:, bass.ds(n, 1), :].rearrange("p a c -> p (a c)")).then_inc(pk_self, 1)
                yield
                dve.wait_ge(pk_self, 1)
                dve.sem_inc(pk_self, -1)

            def pk_dots(c, n):
                dve.wait_ge(gathered[c], n * 256 + 256)
                for r in range(RING):
                    if r == RING // 2:
                        yield
                    down = G[0:ROWS, c, r, 0:C]
                    k = RING * c + r
                    ins = dve.tensor_tensor_reduce(down, down, q_cur[:, :], 1.0, 0.0, ALU.mult, ALU.add,
                                                   xdot[:, k:k + 1])
                ins.then_inc(pk_self, 1)
                yield
                dve.wait_ge(pk_self, 1)
                dve.sem_inc(pk_self, -1)

            def pk_gelu_in(k):
                x = xdot[:, 2 * RING * k:2 * RING * (k + 1)]
                dve.tensor_tensor(gl[:, 0, :], x, x, ALU.mult).then_inc(pk_self, 1)
                yield
                dve.wait_ge(pk_self, 1)
                dve.sem_inc(pk_self, -1)
                dve.tensor_scalar(gl[:, 1, :], gl[:, 0, :], GELU_B, 1.0, ALU.mult, ALU.add).then_inc(pk_self, 1)
                yield
                dve.wait_ge(pk_self, 1)
                dve.sem_inc(pk_self, -1)
                dve.tensor_tensor(gl[:, 0, :], gl[:, 1, :], x, ALU.mult).then_inc(tanh_in, 1)

            def pk_gelu_out(k):
                half = slice(2 * RING * k, 2 * RING * (k + 1))
                dve.wait_ge(tanh_out, 1)
                dve.sem_inc(tanh_out, -1)
                dve.scalar_tensor_tensor(gl[:, 1, :], gl[:, 2, :], 1.0, xdot[:, half], ALU.add, ALU.mult).then_inc(pk_self, 1)
                yield
                dve.wait_ge(pk_self, 1)
                dve.sem_inc(pk_self, -1)
                dve.scalar_tensor_tensor(vals[:, half], gl[:, 1, :], 0.5, w_cur[:, half],
                                         ALU.mult, ALU.mult).then_inc(vals_ready, 1)

            def pk_add(c, n):
                dve.wait_ge(usum_ready, 1)
                dve.sem_inc(usum_ready, -1)
                dve.sem_inc(ring_free[c], 1)
                h_n = h_tok[:, bass.ds(n, 1), :].rearrange("p a c -> p (a c)")
                dve.tensor_tensor(h_n, h_n, sum_bank, ALU.add).then_inc(usum_free, 1)

            def pk_mix_piece(u, n):
                if u == 0:
                    yield from pk_keep(n)
                if u in (0, 1, 4, 5):
                    yield from pk_dots({0: 0, 1: 1, 4: 2, 5: 3}[u], n)
                if u in (1, 5):
                    yield from pk_gelu_in(u // 4)
                if u in (2, 6):
                    yield from pk_gelu_out(u // 4)

            def memory_step(k, b):
                for i, u in mix_steps(k):
                    if u in (4, 5, 8, 9):
                        pk_add({4: 0, 5: 1, 8: 2, 9: 3}[u], b * TPB + i)
                yield
                for i, u in mix_steps(k):
                    yield from pk_mix_piece(u, b * TPB + i)
                i, r = rank_step(k)
                if i is not None:
                    yield from pk_rank_piece(r, (i + 1) % 2)

            def steps(layer, b_mem=None):
                for k in range(STEPS):
                    memory = memory_step(k, b_mem) if b_mem is not None else iter(())
                    if layer == 0 and k < TILES:
                        mask_and_max(k)
                    if layer == 1 and k < TILES:
                        for _ in top16(k):
                            next(memory, None)
                            next(memory, None)
                    for _ in memory:
                        pass

            def attention_out():
                dve.reciprocal(sums[:, :], sums[:, :]).then_inc(dve_ready, 1)
                for j in range(NT // 4):
                    dve.wait_ge(mm_ready_v, 1)
                    dve.sem_inc(mm_ready_v, -1)
                    o_j = o_cm[:, GROUP * j:GROUP * (j + 1)]
                    dve.tensor_tensor(o_j, o_j, bank[j][:, 0:GROUP], ALU.mult).then_inc(dve_ready, 1)
                for j in range(NT // 4):
                    dve.wait_ge(mm_ready_v, 1)
                    dve.sem_inc(mm_ready_v, -1)
                    hj = h_tok[:, 4 * j:4 * j + 4, :]
                    dve.tensor_tensor(hj, hj, bank[j][0:ROWS, :].rearrange("p (k c) -> p k c", k=4), ALU.add)
                meet()

            dve.memset(yT.rearrange("p (b n) -> p b n", b=B)[:, :, T_REAL:T_PAD], 0.0)
            dve.memset(ones_row[:, :], 1.0)
            dve.memset(v_b[:, :, :, :], 1.0)
            dve.memset(xT[:, TOK:TOK + ROWS], 0.0)
            for k in range(3):
                dve.memset(pr[k][:, T_REAL:T_PAD], 0.0)
            for j in range(2 * B):
                b, f = divmod(j, 2)
                at = T_PAD * b + HALF * f
                dve.wait_ge(act_ready, 1)
                dve.sem_inc(act_ready, -1)
                ins = dve.bn_stats(stats[:, j, :], yT[:, at:at + HALF])
            dve.wait_ge(loaded_tok, 16 * 8)
            settle(ins)
            settle(dve.bn_aggr(bn[:, 0:2], stats[:, 0:2 * B, :].rearrange("p j s -> p (j s)")))
            dve.tensor_scalar(bn[:, 2:3], bn[:, 1:2], EPS, None, ALU.add).then_inc(dve_to_act, 1)
            dve.wait_ge(act_ready, 1)
            dve.sem_inc(act_ready, -1)
            settle(dve.reciprocal(bn[:, 3:4], bn[:, 2:3]))
            settle(dve.tensor_tensor(bn[:, 4:5], bn[:, 3:4], col("gamma"), ALU.mult))
            settle(dve.tensor_tensor(bn[:, 5:6], bn[:, 0:1], bn[:, 4:5], ALU.mult))
            settle(dve.tensor_tensor(bn[:, 6:7], col("beta"), bn[:, 5:6], ALU.subtract))
            dve.tensor_scalar(yT, yT, bn[:, 4:5], bn[:, 6:7], ALU.mult, ALU.add).then_inc(dve_ready, 1)
            for j in range(NT // 4):
                dve.wait_ge(mm_ready_v, 1)
                dve.sem_inc(mm_ready_v, -1)
                dve.tensor_copy(h_tok[:, 4 * j:4 * j + 4, :], bank[j][0:ROWS, :].rearrange("p (k c) -> p k c", k=4))
            meet()
            norm_part()
            meet()

            def rotate(bk, rot, bias, bias_sw):
                for f in range(2):
                    half = slice(375 * f, 375 * (f + 1))
                    dve.scalar_tensor_tensor(rot[0][:, half], bank[bk + f][:, 0:375], bias, cosT[:, half],
                                             ALU.add, ALU.mult)
                    ins = dve.scalar_tensor_tensor(rot[1][:, half], bank[bk + 2 + f][:, 0:375], bias_sw,
                                                   sinT[:, half], ALU.add, ALU.mult)
                settle(ins)

            def seen(a):
                return a[:, 2:2 + 3 * PAIRS0].rearrange("p (g r) -> p g r", r=3)[:, :, 0:2]

            def packed(a):
                return a[:, 2:KEYS0].rearrange("p (g r) -> p g r", r=2)

            dve.wait_ge(loaded_all, 16 * N_LOADS)
            settle(dve.memset(KTb, 0.0))
            settle(dve.memset(xc[:, KEYS0:KEYS0_PAD], 0.0))
            for s in range(2):
                dve.sem_inc(slot_free[s], 1)
            with dve.Fori(0, B) as b:
                dve.wait_ge(mm_ready_v, 1)
                dve.sem_inc(mm_ready_v, -1)
                x_b = xT[:, bass.ds(b * T_PAD, T_PAD)]
                dve.tensor_copy(xc[:, 0:2], x_b[:, 0:2])
                dve.tensor_copy(packed(xc), seen(x_b))
                rotate(0, rot_q, col("bq"), col("bqs"))
                dve.tensor_tensor(QTb, *rot_q, ALU.add).then_inc(q_used, 1)
                dve.wait_ge(mm_ready_v, 1)
                dve.sem_inc(mm_ready_v, -1)
                rotate(4, rot_k, col("bk"), col("bks"))
                dve.tensor_tensor(KTb[:, 0:2], rot_k[0][:, 0:2], rot_k[1][:, 0:2], ALU.add)
                settle(dve.tensor_tensor(packed(KTb), seen(rot_k[0]), seen(rot_k[1]), ALU.add))
                dve.sem_inc(qk_here, 1)
                meet()
                steps(0)
                meet()
            meet()
            attention_out()
            norm_part()
            meet()

            def project1(b):
                def h_i(i):
                    return h_tok[:, bass.ds(b * TPB + i, 1), :].rearrange("p a c -> p (a c)")

                for i in range(TPB):
                    ins = dve.bn_stats(stats[0:ROWS, i, :], h_i(i))
                settle(ins)
                for i in range(TPB):
                    ins = dve.bn_aggr(mv[0:ROWS, i, :], stats[0:ROWS, i, :])
                settle(ins)
                dve.tensor_scalar(std[0:ROWS, 0:TPB], mv[0:ROWS, 0:TPB, 1], EPS, None,
                                  ALU.add).then_inc(dve_to_act, 1)
                dve.wait_ge(act_ready, 1)
                dve.sem_inc(act_ready, -1)
                settle(dve.reciprocal(rstd[0:ROWS, 0:TPB], std[0:ROWS, 0:TPB]))
                for i in range(TPB):
                    ins = dve.tensor_scalar(xn_b[:, i, :], h_i(i), mv[0:ROWS, i, 0:1],
                                            rstd[0:ROWS, i:i + 1], ALU.subtract, ALU.mult)
                ins.then_inc(dve_ready, 1)
                dve.wait_ge(act_ready, 1)
                dve.sem_inc(act_ready, -1)
                n = T_REAL
                settle(dve.tensor_scalar(conv_t, xTb, col("conv", 1), col("conv_b"), ALU.mult, ALU.add))
                settle(dve.scalar_tensor_tensor(conv_t[:, 1:n], xTb[:, 0:n - 1], col("conv", 0),
                                                conv_t[:, 1:n], ALU.mult, ALU.add))
                settle(dve.scalar_tensor_tensor(conv_t[:, 0:n - 1], xTb[:, 1:n], col("conv", 2),
                                                conv_t[:, 0:n - 1], ALU.mult, ALU.add))
                dve.tensor_tensor(conv_x, xTb, conv_t, ALU.add).then_inc(dve_ready, 1)
                dve.wait_ge(mm_ready_v, 1)
                dve.sem_inc(mm_ready_v, -1)
                for f in range(2):
                    dve.tensor_copy(v_b[:, :, 3 * f:3 * f + 3, 0:DH].rearrange("p h c d -> p c h d"),
                                    bank[6 + f][0:ROWS, 0:3 * C].rearrange("p (c h d) -> p c h d", c=3, h=H))
                meet()
                for k in range(3):
                    ins = dve.memset(pr[k][:, T_REAL:T_PAD], 0.0)
                settle(ins)

            dve.sem_inc(scores_free, 1)
            dve.sem_inc(usum_free, 1)
            dve.sem_inc(s_free, 1)
            for c in range(4):
                dve.sem_inc(ring_free[c], 1)
            for p in range(2):
                ins = dve.memset(idx[p][:, :], 0)
            settle(ins)
            for r in range(PIECES):
                for _ in pk_rank_piece(r, 0):
                    pass
            steps(None, 0)
            meet()
            project1(0)
            with dve.Fori(1, B) as b:
                steps(1, b)
                meet()
                project1(b)
            dve.sem_inc(memory_done, 1)
            steps(1)
            meet()
            attention_out()
            norm_part()
            dve.wait_ge(mm_ready_v, 1)
            dve.sem_inc(mm_ready_v, -1)
            logits = bank[7][0:ROWS, 0:NT * EXPERTS].rearrange("p (n e) -> p n e", e=EXPERTS)
            full = [ROWS, NT, EXPERTS]
            settle(dve.tensor_reduce(lg_m[:, :], logits, AX.X, ALU.max))
            dve.tensor_tensor(lg[:, :, :], logits, lg_m[:, :].unsqueeze(2).to_broadcast(full),
                              ALU.subtract).then_inc(dve_to_act, 1)
            dve.wait_ge(act_ready, 1)
            dve.sem_inc(act_ready, -1)
            settle(dve.tensor_reduce(lg_m[:, :], lg[:, :, :], AX.X, ALU.add))
            settle(dve.reciprocal(lg_m[:, :], lg_m[:, :]))
            settle(dve.tensor_tensor(lg[:, :, :], lg[:, :, :], lg_m[:, :].unsqueeze(2).to_broadcast(full), ALU.mult))
            for n in range(NT):
                ins = dve.max(top_p[:, n, :], lg[:, n, :])
            settle(ins)
            settle(dve.tensor_tensor(lg_m[:, :], top_p[:, :, 0], top_p[:, :, 1], ALU.add))
            settle(dve.reciprocal(lg_m[:, :], lg_m[:, :]))
            for i in range(2):
                ins = dve.tensor_tensor(p_i[:, i, :], top_p[:, :, i], lg_m[:, :], ALU.mult)
            ins.then_inc(dve_ready, 1)
            settle(dve.tensor_reduce(bn[:, 6:7], cols[:, COL["b2"]:COL["b2"] + EXPERTS], AX.X, ALU.add))
            dve.tensor_scalar(bn[:, 7:8], bn[:, 6:7], 2.0, None, ALU.mult)
            meet()
            dve.sem_inc(chunk_done, FF_RING)
            with dve.Fori(0, TOK // GROUP) as g:
                for m in range(FCH):
                    dve.wait_ge(z_ready, 1)
                    dve.sem_inc(z_ready, -1)
                    dve.wait_ge(chunk_done, 1)
                    dve.sem_inc(chunk_done, -1)
                    dve.tensor_tensor(zg[m % FF_RING], z_bank[m % FF_RING][:, 0:GROUP].unsqueeze(1).to_broadcast([C, 2, GROUP]),
                                      gate[:, :, bass.ds(g * GROUP, GROUP)], ALU.mult).then_inc(zg_ready, 1)
                dve.wait_ge(chunk_done, FF_RING)
                dve.tensor_scalar(yT_ffn, bank[4][:, 0:GROUP], bn[:, 7:8], None, ALU.add).then_inc(dve_ready, 1)
                dve.wait_ge(mm_ready_v, 1)
                dve.sem_inc(mm_ready_v, -1)
                h_g = h_tok[:, bass.ds(g * 4, 4), :]
                dve.tensor_tensor(h_g, h_g, bank[5][0:ROWS, :].rearrange("p (k c) -> p k c", k=4), ALU.add)
            meet()
            dve.sem_inc(h_done, 1)

        @block.gpsimd
        def _(pool):
            with pool.Fori(0, NT // 2):
                for p in range(2):
                    pool.wait_ge(idx_ready, 1)
                    pool.sem_inc(idx_ready, -1)
                    for c in range(4):
                        pool.wait_ge(ring_free[c], 1)
                        pool.sem_inc(ring_free[c], -1)
                        for r in range(RING):
                            k = RING * c + r
                            pool.indirect_dma_start(
                                out=G[:, c, r, :], out_offset=None, in_=t["tables"],
                                in_offset=bass.IndirectOffsetOnAxis(ap=idx[p][:, k:k + 1], axis=0),
                            ).then_inc(gathered[c], 16)
            with pool.Fori(0, TOK // GROUP):
                for m in range(FCH):
                    pool.wait_ge(g_ready, 1)
                    pool.sem_inc(g_ready, -1)
                    pool.tensor_tensor(g_sum[m % FF_RING], zg[m % FF_RING][:, 0, :], zg[m % FF_RING][:, 1, :],
                                       ALU.add).then_inc(gs_ready, 1)

def layouts(inputs):
    import numpy as np
    a = {k: np.asarray(v) for k, v in inputs.items()}
    swap = np.arange(C).reshape(-1, 2)[:, ::-1].reshape(-1)
    d = {}
    d["x"] = a["x"].transpose(2, 0, 1)
    d["tok_W"] = a["L0_tok_W"].T
    d["cols"] = np.concatenate(
        [a["L0_tok_b"][:, None], a["L0_tok_gamma"][:, None], a["L0_tok_beta"][:, None],
         a["L0_attn_bq"][:, None], a["L0_attn_bq"][swap][:, None],
         a["L0_attn_bk"][:, None], a["L0_attn_bk"][swap][:, None],
         a["L1_attn_conv_w"][:, 0, :], a["L1_attn_conv_b"][:, None],
         a["L1_attn_b_qkv"][0:C][:, None], a["L1_attn_b_qkv"][C:2 * C][:, None],
         a["L0_ffn_bq"].reshape(PK_HEADS, C).T, a["L1_ffn_b1"].reshape(FCH, C).T,
         a["L1_ffn_b2"].T, a["L1_ffn_b2"].T[:, 0:3]], axis=1)
    d["ident"] = np.eye(C, dtype=np.float32)
    d["iota8"] = np.broadcast_to(np.arange(PK_TOP, dtype=np.float32), (C, PK_TOP))
    d["a0w"] = np.stack([a["L0_attn_Wq"], a["L0_attn_Wq"][:, swap], a["L0_attn_Wk"], a["L0_attn_Wk"][:, swap],
                         a["L0_attn_Wv"], a["L0_attn_Wo"]], axis=1)
    d["rows1"] = np.stack([a["L0_attn_bv"], a["L0_attn_bo"], a["L1_attn_b_qkv"][2 * C:], a["L1_attn_b_o"]])[None]
    inv_freq = (np.float32(1.0) / np.float32(10000.0) ** (np.arange(0, C, 2, dtype=np.float32) / np.float32(C)))
    ang = np.repeat(inv_freq.astype(np.float32)[:, None] * np.arange(T_PAD, dtype=np.float32)[None, :], 2, axis=0)
    sign = np.where(np.arange(C) % 2 == 0, -1.0, 1.0).astype(np.float32)[:, None]
    d["cosT"] = np.cos(ang).astype(np.float32)
    d["sinT"] = (np.sin(ang) * sign).astype(np.float32)
    g = np.arange(PAIRS0)
    key = np.concatenate([[0, 1], np.stack([3 * g + 2, 3 * g + 3], axis=1).reshape(-1), [T_PAD, T_PAD]])
    tok = np.arange(T_PAD).reshape(TPB, ROWS)
    d["mask0"] = np.where(key[None, None, :] <= tok.T[:, :, None], 0.0, NEG).astype(np.float32)
    d["pkwq"] = a["L0_ffn_Wq"].T
    d["pkkeys"] = a["L0_ffn_keys"].transpose(1, 3, 0, 2).reshape(C, PK_HEADS * C)
    d["tables"] = np.concatenate([a["L0_ffn_w_down_embed"], a["L0_ffn_w_up_embed"]], axis=1)
    wqkv = a["L1_attn_w_qkv"]
    d["a1w"] = np.stack([wqkv[:, 0:C], wqkv[:, C:2 * C], wqkv[:, 2 * C:], a["L1_attn_w_o"]], axis=1)
    head_of = np.arange(C) // DH
    d["spread"] = (np.arange(TPB * H)[:, None, None] == np.arange(TPB)[None, :, None] * H
                   + head_of[None, None, :]).astype(np.float32)
    d["Wg"] = a["L1_ffn_Wg"]
    d["W1"] = a["L1_ffn_W1"].transpose(1, 0, 2).reshape(C, FCH, C)
    d["W2"] = a["L1_ffn_W2"].reshape(FCH, C, C).transpose(1, 0, 2)
    return {k: np.ascontiguousarray(v) for k, v in d.items()}


def kernel(**inputs):
    import concourse.bacc as bacc
    from concourse.bass_utils import run_bass_kernel_spmd

    arrays = {f"in_{k}": v for k, v in layouts(inputs).items()}
    nc = bacc.Bacc("TRN2", target_bir_lowering=False, num_devices=1)
    t = {k.removeprefix("in_"): nc.dram_tensor(k, v.shape, mybir.dt.from_np(v.dtype), kind="ExternalInput").ap()
         for k, v in arrays.items()}
    t["out"] = nc.dram_tensor("out", (B, T_REAL, C), F32, kind="ExternalOutput").ap()
    audio_tower(nc, t)
    r = run_bass_kernel_spmd(nc, [arrays], core_ids=[0])
    return r.results[0]["out"]
```
